# Optimizing a Trainium2 kernel written in Bass

```python
import numpy as np
import jax
import jax.numpy as jnp

def _softmax(x, axis=-1):
    return jax.nn.softmax(x, axis=axis)

def _gelu(x):
    return jax.nn.gelu(x, approximate=True)

def _silu(x):
    return jax.nn.silu(x)

def _sigmoid(x):
    return jax.nn.sigmoid(x)

def _layernorm(x, axis=-1, eps=1e-05):
    m = jnp.mean(x, axis=axis, keepdims=True)
    v = jnp.var(x, axis=axis, keepdims=True)
    return (x - m) / jnp.sqrt(v + eps)

def _scatter_add(tgt, idx, src, axis=0):
    return tgt.at[idx].add(src)

def _segment_sum(src, seg, n):
    return jax.ops.segment_sum(src, seg, n)
kernel_name = 'mk_cond_seq_d2_seqx_r4_2eda0f'

def setup_inputs(seed: int=0):
    np.random.seed(seed)
    _w = jnp.asarray

    def _rec_inputs():
        import jax
        import jax.numpy as jnp
        _rk = jax.random.key(seed)
        x = -7.109e-05 + 0.9999 * jax.random.normal(jax.random.fold_in(_rk, 1), (128, 64, 256), jnp.float32)
        _lenS = 64 - jax.random.randint(jax.random.fold_in(_rk, 7), (128,), 0, max(1, 64 // 4) + 1, jnp.int32)
        _lenS2 = 64 - jax.random.randint(jax.random.fold_in(_rk, 8), (128,), 0, max(1, 64 // 4) + 1, jnp.int32)
        itok_B_0_2 = jax.random.randint(jax.random.fold_in(_rk, 11), (128,), 0, 3, jnp.int32)
        itok_B_0_15 = jax.random.randint(jax.random.fold_in(_rk, 12), (128,), 0, 16, jnp.int32)
        return (x, itok_B_0_2, itok_B_0_15)
    x, itok_B_0_2, itok_B_0_15 = _rec_inputs()

    def _L0_cond_setup():
        import jax, jax.numpy as jnp
        import numpy as np
        H = 256
        EPS = 1e-05

        def _gelu(x):
            return jax.nn.gelu(x, approximate=False)
        key = jax.random.key(seed)
        ks = jax.random.split(key, 16)
        s = 1.0 / np.sqrt(H)
        inp = {'x': jax.random.normal(ks[0], (64, 256, H), dtype=jnp.float32), 'condition': jax.random.randint(ks[1], (64,), 0, 3), 'w1_nr': jax.random.normal(ks[2], (H, H), dtype=jnp.float32) * s, 'b1_nr': jnp.zeros((H,), dtype=jnp.float32), 'w2_nr': jax.random.normal(ks[3], (H, H), dtype=jnp.float32) * s, 'b2_nr': jnp.zeros((H,), dtype=jnp.float32), 'w1_tsr': jax.random.normal(ks[4], (H, H), dtype=jnp.float32) * s, 'b1_tsr': jnp.zeros((H,), dtype=jnp.float32), 'w2_tsr': jax.random.normal(ks[5], (H, H), dtype=jnp.float32) * s, 'b2_tsr': jnp.zeros((H,), dtype=jnp.float32), 'w1_sr': jax.random.normal(ks[6], (H, 2 * H), dtype=jnp.float32) * s, 'b1_sr': jnp.zeros((2 * H,), dtype=jnp.float32), 'w2_sr': jax.random.normal(ks[7], (2 * H, H), dtype=jnp.float32) * (1.0 / np.sqrt(2 * H)), 'b2_sr': jnp.zeros((H,), dtype=jnp.float32), 'w3_sr': jax.random.normal(ks[8], (H, H), dtype=jnp.float32) * s, 'b3_sr': jnp.zeros((H,), dtype=jnp.float32), 'gamma': jnp.ones((H,), dtype=jnp.float32), 'beta': jnp.zeros((H,), dtype=jnp.float32)}
        return inp
    _L0_cond_all = _L0_cond_setup()
    _L0_cond_in = {k: v for k, v in _L0_cond_all.items() if k in ('w1_nr', 'b1_nr', 'w2_nr', 'b2_nr', 'w1_tsr', 'b1_tsr', 'w2_tsr', 'b2_tsr', 'w1_sr', 'b1_sr', 'w2_sr', 'b2_sr', 'w3_sr', 'b3_sr', 'gamma', 'beta')}
    del _L0_cond_all

    def _L1_cond_setup():
        import jax, jax.numpy as jnp
        import numpy as np
        B, S, D = (32, 256, 256)
        A = 64
        E = 16
        LN_EPS = 1e-05
        key = jax.random.key(seed)
        ks = jax.random.split(key, 10)
        s = lambda fan_in: 1.0 / np.sqrt(fan_in)
        return {'hidden_states': jax.random.normal(ks[0], (B, S, D), dtype=jnp.float32), 'domain_id': jax.random.randint(ks[1], (B,), 0, E, dtype=jnp.int64), 'down_W': jax.random.uniform(ks[2], (A, D), jnp.float32, -s(D), s(D)), 'down_b': jax.random.uniform(ks[3], (A,), jnp.float32, -s(D), s(D)), 'up_W': jax.random.uniform(ks[4], (D, A), jnp.float32, -s(A), s(A)), 'up_b': jax.random.uniform(ks[5], (D,), jnp.float32, -s(A), s(A)), 'expert_W': jax.random.uniform(ks[6], (E, A, A), jnp.float32, -s(A), s(A)), 'expert_b': jax.random.uniform(ks[7], (E, A), jnp.float32, -s(A), s(A)), 'domain_emb': jax.random.normal(ks[8], (E, A), dtype=jnp.float32), 'ln_gamma': jnp.ones((D,), jnp.float32), 'ln_beta': jnp.zeros((D,), jnp.float32)}
    _L1_cond_all = _L1_cond_setup()
    _L1_cond_in = {k: v for k, v in _L1_cond_all.items() if k in ('down_W', 'down_b', 'up_W', 'up_b', 'expert_W', 'expert_b', 'domain_emb', 'ln_gamma', 'ln_beta')}
    del _L1_cond_all
    return {'x': x, 'itok_B_0_2': itok_B_0_2, 'itok_B_0_15': itok_B_0_15, 'L0_cond_w1_nr': _L0_cond_in['w1_nr'], 'L0_cond_b1_nr': _L0_cond_in['b1_nr'], 'L0_cond_w2_nr': _L0_cond_in['w2_nr'], 'L0_cond_b2_nr': _L0_cond_in['b2_nr'], 'L0_cond_w1_tsr': _L0_cond_in['w1_tsr'], 'L0_cond_b1_tsr': _L0_cond_in['b1_tsr'], 'L0_cond_w2_tsr': _L0_cond_in['w2_tsr'], 'L0_cond_b2_tsr': _L0_cond_in['b2_tsr'], 'L0_cond_w1_sr': _L0_cond_in['w1_sr'], 'L0_cond_b1_sr': _L0_cond_in['b1_sr'], 'L0_cond_w2_sr': _L0_cond_in['w2_sr'], 'L0_cond_b2_sr': _L0_cond_in['b2_sr'], 'L0_cond_w3_sr': _L0_cond_in['w3_sr'], 'L0_cond_b3_sr': _L0_cond_in['b3_sr'], 'L0_cond_gamma': _L0_cond_in['gamma'], 'L0_cond_beta': _L0_cond_in['beta'], 'L1_cond_down_W': _L1_cond_in['down_W'], 'L1_cond_down_b': _L1_cond_in['down_b'], 'L1_cond_up_W': _L1_cond_in['up_W'], 'L1_cond_up_b': _L1_cond_in['up_b'], 'L1_cond_expert_W': _L1_cond_in['expert_W'], 'L1_cond_expert_b': _L1_cond_in['expert_b'], 'L1_cond_domain_emb': _L1_cond_in['domain_emb'], 'L1_cond_ln_gamma': _L1_cond_in['ln_gamma'], 'L1_cond_ln_beta': _L1_cond_in['ln_beta']}

def reference(x, itok_B_0_2, itok_B_0_15, L0_cond_w1_nr, L0_cond_b1_nr, L0_cond_w2_nr, L0_cond_b2_nr, L0_cond_w1_tsr, L0_cond_b1_tsr, L0_cond_w2_tsr, L0_cond_b2_tsr, L0_cond_w1_sr, L0_cond_b1_sr, L0_cond_w2_sr, L0_cond_b2_sr, L0_cond_w3_sr, L0_cond_b3_sr, L0_cond_gamma, L0_cond_beta, L1_cond_down_W, L1_cond_down_b, L1_cond_up_W, L1_cond_up_b, L1_cond_expert_W, L1_cond_expert_b, L1_cond_domain_emb, L1_cond_ln_gamma, L1_cond_ln_beta):
    import jax
    import jax.numpy as jnp

    def _L0_cond_ref(x, condition, w1_nr, b1_nr, w2_nr, b2_nr, w1_tsr, b1_tsr, w2_tsr, b2_tsr, w1_sr, b1_sr, w2_sr, b2_sr, w3_sr, b3_sr, gamma, beta):
        import jax, jax.numpy as jnp
        import numpy as np
        H = 256
        EPS = 1e-05

        def _gelu(x):
            return jax.nn.gelu(x, approximate=False)
        out_nr = _gelu(jnp.einsum('bth,hk->btk', x, w1_nr) + b1_nr)
        out_nr = jnp.einsum('bth,hk->btk', out_nr, w2_nr) + b2_nr
        out_tsr = _gelu(jnp.einsum('bth,hk->btk', x, w1_tsr) + b1_tsr)
        out_tsr = jnp.einsum('bth,hk->btk', out_tsr, w2_tsr) + b2_tsr
        h = _gelu(jnp.einsum('bth,hk->btk', x, w1_sr) + b1_sr)
        h = _gelu(jnp.einsum('bth,hk->btk', h, w2_sr) + b2_sr)
        out_sr = jnp.einsum('bth,hk->btk', h, w3_sr) + b3_sr
        c = condition[:, None, None]
        out = jnp.where(c == 0, out_nr, jnp.where(c == 1, out_tsr, jnp.where(c == 2, out_sr, jnp.zeros_like(x))))
        y = x + out
        mu = jnp.mean(y, axis=-1, keepdims=True)
        var = jnp.mean((y - mu) ** 2, axis=-1, keepdims=True)
        return (y - mu) * jax.lax.rsqrt(var + EPS) * gamma + beta

    def _L1_cond_ref(hidden_states, domain_id, down_W, down_b, up_W, up_b, expert_W, expert_b, domain_emb, ln_gamma, ln_beta):
        import jax, jax.numpy as jnp
        import numpy as np
        B, S, D = (32, 256, 256)
        A = 64
        E = 16
        LN_EPS = 1e-05
        residual = hidden_states
        hidden = jnp.einsum('bsd,ad->bsa', hidden_states, down_W) + down_b
        hidden = jax.nn.gelu(hidden, approximate=False)
        valid = (domain_id >= 0) & (domain_id < E)
        idx = jnp.clip(domain_id, 0, E - 1)
        Wsel = expert_W[idx]
        bsel = expert_b[idx]
        expert_out = jnp.einsum('bsa,boa->bso', hidden, Wsel) + bsel[:, None, :]
        domain_output = jnp.where(valid[:, None, None], expert_out, hidden)
        hidden = domain_output + domain_emb[idx][:, None, :]
        hidden = jnp.einsum('bsa,da->bsd', hidden, up_W) + up_b
        x = hidden + residual
        mu = jnp.mean(x, axis=-1, keepdims=True)
        var = jnp.mean(jnp.square(x - mu), axis=-1, keepdims=True)
        return (x - mu) * jax.lax.rsqrt(var + LN_EPS) * ln_gamma + ln_beta
    x = _L0_cond_ref(x, itok_B_0_2, L0_cond_w1_nr, L0_cond_b1_nr, L0_cond_w2_nr, L0_cond_b2_nr, L0_cond_w1_tsr, L0_cond_b1_tsr, L0_cond_w2_tsr, L0_cond_b2_tsr, L0_cond_w1_sr, L0_cond_b1_sr, L0_cond_w2_sr, L0_cond_b2_sr, L0_cond_w3_sr, L0_cond_b3_sr, L0_cond_gamma, L0_cond_beta)
    x = _L1_cond_ref(x, itok_B_0_15, L1_cond_down_W, L1_cond_down_b, L1_cond_up_W, L1_cond_up_b, L1_cond_expert_W, L1_cond_expert_b, L1_cond_domain_emb, L1_cond_ln_gamma, L1_cond_ln_beta)
    return x

_drawn_inputs = setup_inputs


def setup_inputs(seed=0):
    import zlib

    import numpy as np

    out = dict(_drawn_inputs(seed))
    spreads = {'L0_cond_b1_nr': (0.0, 0.1),
     'L0_cond_b2_nr': (0.0, 0.1),
     'L0_cond_b1_tsr': (0.0, 0.1),
     'L0_cond_b2_tsr': (0.0, 0.1),
     'L0_cond_b1_sr': (0.0, 0.438),
     'L0_cond_b2_sr': (0.0, 0.298),
     'L0_cond_b3_sr': (0.0, 0.1),
     'L0_cond_gamma': (1.0, 0.2),
     'L0_cond_beta': (0.0, 0.1),
     'L1_cond_ln_gamma': (1.0, 0.2),
     'L1_cond_ln_beta': (0.0, 0.1)}
    factors = {'L1_cond_down_b': 8.0}
    for name, (base, spread) in spreads.items():
        noise = np.random.default_rng([zlib.crc32(name.encode()), seed]).standard_normal(out[name].shape)
        drawn = base * np.exp(spread * noise) if base else spread * noise
        out[name] = jnp.asarray(drawn.astype(out[name].dtype))
    for name, factor in factors.items():
        out[name] = (out[name] * factor).astype(out[name].dtype)
    return out
```

```python
from contextlib import ExitStack

import concourse.bass as bass
from concourse import mybir

F32 = mybir.dt.float32
F32R = mybir.dt.float32r
I32 = mybir.dt.int32
ALU = mybir.AluOpType
ACT = mybir.ActivationFunctionType
AX = mybir.AxisListType

P = 128
EPS = 1e-5

SR, NR, TSR, OTHER = range(4)
KINDS = 4
ROW_B_SR, ROW_B_NR, ROW_B_TSR, ROW_G1, ROW_G2, ROW_BETA1, ROW_BETA2 = range(7)
ROWS = 7
COL_B1_NR, COL_B1_TSR, COL_B1_SR, COL_B2_SR, COL_G1, COL_BETA1, COL_DOWN_B, COLS = 0, 2, 4, 8, 10, 12, 14, 15


def conditioned_layers(nc, x_tok, x_feat, cond, dom, w1_nr, w2_nr, w1_tsr, w2_tsr, w1_sr, w2_sr, w3_sr,
                       cols, rows, down_t, up_b1, expert_t, expert_b_t, emb_t, out):
    B, T, H = x_tok.shape
    KC = H // P
    A = down_t.shape[-1]
    E = expert_t.shape[1]
    TE = E + 2
    G = 4
    N = G * T
    TT = N // P
    S_MIN = B // G
    S_MAX = S_MIN + KINDS - 1
    POS = (S_MAX + 1) * G
    WIDTH = POS + 6 * G
    NO_STORE = 1000
    assert B == P and 2 * T == P and 2 * A == P and TT == 2 and KC == 2

    scratch = nc.dram_tensor("padding_rows", [WIDTH, T, H], F32, kind="Internal").ap()

    with ExitStack() as ctx:
        def sb(name, shape, dt=F32):
            return ctx.enter_context(nc.sbuf_tensor(name, shape, dt))

        def ps(name, shape):
            return ctx.enter_context(nc.psum_tensor(name, shape, F32))

        def sem(name):
            return ctx.enter_context(nc.semaphore(name))

        W1 = {NR: sb("w1_nr_sb", [P, KC, H]), TSR: sb("w1_tsr_sb", [P, KC, H]), SR: sb("w1_sr_sb", [P, KC, 2 * H])}
        W2 = {NR: sb("w2_nr_sb", [P, KC, H]), TSR: sb("w2_tsr_sb", [P, KC, H]), SR: sb("w2_sr_sb", [P, 2 * KC, H])}
        W3 = sb("w3_sr_sb", [P, KC, H])
        COL = sb("col_sb", [P, COLS])
        ROW = sb("row_sb", [P, ROWS, H])
        DT = sb("down_t_sb", [P, KC, A])
        UPB = sb("up_b_sb", [A + 1, H])
        EXP = sb("expert_sb", [A, TE, 2, A])
        EB = sb("expert_b_sb", [A, E])
        EM = sb("emb_sb", [A, E])
        CONDI = sb("cond_i", [P, 1], I32)
        DOMI = sb("dom_i", [P, 1], I32)
        ident = sb("ident", [P, P])
        before = sb("before", [P, P])
        ones = sb("ones", [P, P])
        zeros = sb("zeros", [P, 2 * H])
        seq_no = sb("seq_no", [P, 1])
        pos_no = sb("pos_no", [P, POS])
        sc = sb("sort_scratch", [P, 40])
        kind1 = sb("kind_onehot", [P, KINDS])
        start = sb("kind_start", [P, KINDS + 1])
        nslot_i = sb("kind_slots_i", [P, KINDS], I32)
        nslot_s = sb("kind_slots_s", [P, KINDS], I32)
        val3 = sb("values", [P, 3])
        place = sb("place", [P, POS])
        IDS = sb("ids", [1, 3, WIDTH], I32)
        BND = sb("bounds", [1, KINDS], I32)
        D0 = sb("down_dup", [P, KC, 2, A])
        DG = sb("down_gain_dup", [P, KC, 2, A])
        BD = sb("down_bias", [P, 1])
        BE = sb("expert_const", [A + 1, TE])
        CH = sb("const_hi", [TE, H], F32R)
        CL = sb("const_lo", [TE, H], F32R)
        T1 = sb("table_hi", [P, TE * H], F32R)
        T2 = sb("table_lo", [A + 2, TE * H], F32R)
        mhalf = sb("minus_half", [P, TT])
        XF = [sb(f"x_feat{p}", [P, G, KC, T]) for p in range(2)]
        X = [sb(f"x_tok{p}", [P, TT, H]) for p in range(2)]
        h1 = sb("h1", [P, 2 * KC, N])
        h2 = sb("h2", [P, KC, N])
        Z = [sb(f"z{p}", [P, TT, H]) for p in range(2)]
        ZN = sb("zn", [P, TT, H])
        Y = [sb(f"y{p}", [P, TT, H]) for p in range(2)]
        YT = sb("yt", [P, KC, N])
        GF = sb("gelu_f", [P, N])
        S = sb("stack", [P, TT, 3, T], F32R)
        X2 = sb("stack_hi", [A + 2, TT, 3, T], F32R)
        Z2 = [sb(f"zz{p}", [P, TT, H]) for p in range(2)]
        N2 = [sb(f"nn{p}", [P, TT, H]) for p in range(2)]
        O = [sb(f"o{p}", [P, TT, H]) for p in range(2)]
        ST = [[sb(f"st{n}{p}", [P, TT, 6]) for p in range(2)] for n in range(2)]
        MV = [[sb(f"mv{n}{p}", [P, TT, 2]) for p in range(2)] for n in range(2)]
        VE = [[sb(f"ve{n}{p}", [P, TT]) for p in range(2)] for n in range(2)]
        RS = [[sb(f"rs{n}{p}", [P, TT]) for p in range(2)] for n in range(2)]
        NM = [[sb(f"nm{n}{p}", [P, TT]) for p in range(2)] for n in range(2)]

        H0 = ps("ps_h0", [P, 2, N])
        H1 = ps("ps_h1", [P, 2, N])
        H2 = ps("ps_h2", [P, 2, N])
        ZP = [ps(f"ps_z{t}", [P, 2 * H]) for t in range(TT)]
        TP = ps("ps_t", [P, KC, N])
        DP = ps("ps_d", [P, 2 * N])
        UP = ps("ps_u", [P, TT, H])

        s_ids_in = sem("s_ids_in")
        s_row_in = sem("s_row_in")
        s_w_in = sem("s_w_in")
        s_e_in = sem("s_e_in")
        s_const = sem("s_const")
        s_prep = sem("s_prep")
        s_kinds = sem("s_kinds")
        s_placed = sem("s_placed")
        s_weights = sem("s_weights")
        s_rank = sem("s_rank")
        s_ids_ps = sem("s_ids_ps")
        s_tables = sem("s_tables")
        s_bias_ps = sem("s_bias_ps")
        s_const_ps = sem("s_const_ps")
        s_ct = sem("s_ct")
        s_ct_in = sem("s_ct_in")
        s_fold = sem("s_fold")
        s_fold_hi = sem("s_fold_hi")
        s_fold_lo = sem("s_fold_lo")
        s_prep_done = sem("s_prep_done")
        ld_xf = [sem(f"ld_xf{p}") for p in range(2)]
        ld_x = [sem(f"ld_x{p}") for p in range(2)]
        st_out = [sem(f"st_out{p}") for p in range(2)]
        out_free = sem("out_free")
        h0_ps = sem("h0_ps")
        h1_ps = sem("h1_ps")
        h2_ps = sem("h2_ps")
        h0_act = sem("h0_act")
        h1_act = sem("h1_act")
        h2_act = sem("h2_act")
        z_ps = [sem(f"z_ps{t}") for t in range(TT)]
        z_made = sem("z_made")
        z_free = sem("z_free")
        xb = sem("xb")
        stat = [sem("stat1"), sem("stat2")]
        stats_seen = sem("stats_seen")
        var = [sem("var1"), sem("var2")]
        rstd = [sem("rstd1"), sem("rstd2")]
        nmr = [sem("nmr1"), sem("nmr2")]
        zn_act = sem("zn_act")
        y_mul = sem("y_mul")
        y_done = sem("y_done")
        t_ps = sem("t_ps")
        yt_act = sem("yt_act")
        d_ps = sem("d_ps")
        g_act = sem("g_act")
        lo_made = sem("lo_made")
        s_made = sem("s_made")
        u_ps = sem("u_ps")
        z2_free = sem("z2_free")
        n2_act = sem("n2_act")
        o_mul = sem("o_mul")
        o_made = sem("o_made")

        HEAD, MAIN, TAIL = "head", "main", "tail"
        HEAD_STEPS = 4
        TAIL_START = S_MIN - S_MIN % 2 - 2
        LAST_STEP = S_MAX + 4

        def steps(eng):
            for g in range(HEAD_STEPS):
                yield g, g // 2, g % 2, HEAD
            for first, last, where in ((HEAD_STEPS, TAIL_START, MAIN), (TAIL_START, LAST_STEP + 1, TAIL)):
                with eng.Fori(first // 2, last // 2) as i:
                    for p in range(2):
                        yield 2 * i + p, i, p, where

        def on_slot(eng, g, lag, where, n_slots):
            if where == TAIL:
                with eng.If(g < n_slots + lag):
                    yield g - lag
            elif where == MAIN or g >= lag:
                yield g - lag

        def bounds(eng):
            eng.wait_ge(s_tables, 1)
            return [eng.value_load(BND[0:1, k:k + 1], min_val=0, max_val=S_MAX) for k in range(KINDS)]

        def four(eng, row, slot, top):
            _, v = nc.values_load_multi_w_load_instructions(
                IDS[0:1, row, bass.ds(slot * G, G)], engines=[eng.engine], min_val=0, max_val=top,
                skip_runtime_bounds_check_because="the entries are worked out from one-hot sums")
            return v

        def pair_cols(tile):
            return tile[:, :, 0:3:2, :]

        block = ctx.enter_context(nc.Block())

        @block.sync
        def _(sp):
            sp.dma_start(CONDI[:, :], cond).then_inc(s_ids_in, 16)
            sp.dma_start(DOMI[:, :], dom).then_inc(s_ids_in, 16)
            for dst, src in ((W1[SR], w1_sr), (W1[NR], w1_nr), (W1[TSR], w1_tsr),
                             (W2[SR], w2_sr), (W2[NR], w2_nr), (W2[TSR], w2_tsr), (W3, w3_sr)):
                sp.dma_start(dst[:, :, :], src.rearrange("(c p) n -> p c n", p=P)).then_inc(s_w_in, 16)

            def load_feat(slot, p, tile_free):
                ids = four(sp, 0, slot, B - 1)
                tile_free()
                for k in range(G):
                    src = x_feat[bass.ds(ids[k], 1), :, :, :].rearrange("a p c t -> (a p) c t")
                    sp.dma_start(XF[p][:, k, :, :], src).then_inc(ld_xf[p], 16)
                return ids

            def load_tok(ids, p):
                for k in range(G):
                    src = x_tok[bass.ds(ids[k], 1), :, :].rearrange("a t n -> (a t) n")
                    half = slice(T * (k % 2), T * (k % 2) + T)
                    sp.dma_start(X[p][half, k // 2, :], src).then_inc(ld_x[p], 16)

            n_slots = bounds(sp)[OTHER]
            for p in range(2):
                ids = load_feat(p, p, lambda: None)
                load_tok(ids, p)
            sp.sem_inc(out_free, 2)
            for g, i, p, where in steps(sp):
                for _ in on_slot(sp, g, -2, where, n_slots):
                    load_feat(g + 2, p, lambda: sp.wait_ge(h1_ps, g + 1))
                for _ in on_slot(sp, g, 3, where, n_slots):
                    q = 1 - p
                    ids = four(sp, 1, g - 3, B - 1 + NO_STORE)
                    for k in range(G):
                        src = O[q][T * (k % 2):T * (k % 2) + T, k // 2, :]
                        with sp.If(ids[k] < B):
                            stored = nc.s_assert_within(ids[k], 0, B - 1, skip_runtime_bounds_check_because="the branch tests it")
                            sp.wait_ge(o_made, g - 2)
                            sp.dma_start(out[bass.ds(stored, 1), :, :].rearrange("a t n -> (a t) n"),
                                         src).then_inc(st_out[q], 16)
                        with sp.Else():
                            sp.wait_ge(o_made, g - 2)
                            sp.dma_start(scratch[bass.ds((g - 3) * G + k, 1), :, :].rearrange("a t n -> (a t) n"),
                                         src).then_inc(st_out[q], 16)
                for _ in on_slot(sp, g, -2, where, n_slots):
                    ids = four(sp, 0, g + 2, B - 1)
                    sp.wait_ge(z_free, g + 2)
                    load_tok(ids, p)
                for _ in on_slot(sp, g, 4, where, n_slots):
                    sp.wait_ge(st_out[p], 16 * G * (i - 1))
                    sp.sem_inc(out_free, 1)

        @block.gpsimd
        def _(pool):
            pool.memset(ones[:, :], 1.0)
            pool.memset(ident[:, :], 0.0).then_inc(s_const, 1)
            pool.wait_ge(s_const, 1)
            pool.affine_select(out=ident[:, :], in_=ident[:, :], compare_op=ALU.not_equal, fill=1.0, base=0,
                               pattern=[[-1, P]], channel_multiplier=1).then_inc(s_const, 1)
            pool.affine_select(out=before[:, :], in_=ones[:, :], compare_op=ALU.is_gt, fill=0.0, base=0,
                               pattern=[[1, P]], channel_multiplier=-1)
            pool.iota(seq_no[:, :], pattern=[[0, 1]], base=0, channel_multiplier=1,
                      allow_small_or_imprecise_dtypes=True)
            pool.iota(pos_no[:, :], pattern=[[1, POS]], base=0, channel_multiplier=0,
                      allow_small_or_imprecise_dtypes=True)
            pool.memset(mhalf[:, :], -0.5).then_inc(s_const, 1)
            pool.dma_start(EXP[:, 0:E, 0, :], expert_t).then_inc(s_e_in, 16)
            pool.dma_start(EXP[:, 0:E, 1, :], expert_t).then_inc(s_e_in, 16)
            pool.dma_start(UPB[:, :], up_b1).then_inc(s_e_in, 16)
            pool.dma_start(EB[:, :], expert_b_t).then_inc(s_e_in, 16)
            pool.dma_start(EM[:, :], emb_t).then_inc(s_e_in, 16)
            pool.dma_start(DT[:, :, :], down_t).then_inc(s_e_in, 16)
            pool.dma_start(COL[:, :], cols).then_inc(s_row_in, 16)
            pool.dma_start(ROW[:, :, :], rows.partition_broadcast(P)).then_inc(s_row_in, 16)
            pool.wait_ge(s_row_in, 32)
            b_sr, b_nr, b_tsr, n_slots = bounds(pool)

            def both(row):
                return ROW[:, row, :].unsqueeze(1).to_broadcast([P, TT, H])

            def power(n, slot, p):
                pool.wait_ge(var[n], slot + 1)
                pool.tensor_tensor(RS[n][p][:, :], VE[n][p][:, :], mhalf[:, :], ALU.pow).then_inc(rstd[n], 1)

            for g, i, p, where in steps(pool):
                q = 1 - p
                for _ in on_slot(pool, g, 0, where, n_slots):
                    def add_bias(row):
                        pool.wait_ge(ld_x[p], 16 * G * (i + 1))
                        pool.tensor_tensor(X[p][:, :, :], X[p][:, :, :], both(row), ALU.add).then_inc(xb, 1)

                    with pool.If(g < b_sr):
                        add_bias(ROW_B_SR)
                    with pool.Else():
                        with pool.If(g < b_nr):
                            add_bias(ROW_B_NR)
                        with pool.Else():
                            with pool.If(g < b_tsr):
                                add_bias(ROW_B_TSR)
                            with pool.Else():
                                pool.wait_ge(ld_x[p], 16 * G * (i + 1))
                                pool.tensor_tensor(X[p][:, :, :], X[p][:, :, :],
                                                   zeros[:, :].rearrange("p (t n) -> p t n", t=TT),
                                                   ALU.add).then_inc(xb, 1)
                for _ in on_slot(pool, g, 1, where, n_slots):
                    pool.wait_ge(zn_act, g)
                    pool.tensor_tensor(Y[q][:, :, :], ZN[:, :, :], both(ROW_G1), ALU.mult).then_inc(y_mul, 1)
                for _ in on_slot(pool, g, 2, where, n_slots):
                    power(1, g - 2, p)
                for _ in on_slot(pool, g, 1, where, n_slots):
                    pool.wait_ge(y_mul, g)
                    pool.tensor_tensor(Y[q][:, :, :], Y[q][:, :, :], both(ROW_BETA1), ALU.add).then_inc(y_done, 1)
                for _ in on_slot(pool, g, 0, where, n_slots):
                    power(0, g, p)

        @block.vector
        def _(dve):
            done = [0]

            def step(ins):
                done[0] += 1
                ins.then_inc(s_prep, 1)
                dve.wait_ge(s_prep, done[0])

            C, D, LO, HI = sc[:, 0:1], sc[:, 1:2], sc[:, 2:3], sc[:, 3:4]
            step(dve.memset(zeros[:, :], 0.0))
            dve.wait_ge(s_const, 3)
            dve.wait_ge(s_ids_in, 32)
            step(dve.tensor_copy(C, CONDI[:, :]))
            step(dve.tensor_copy(D, DOMI[:, :]))
            step(dve.tensor_scalar(kind1[:, SR:SR + 1], C, 2.0, None, ALU.is_equal))
            step(dve.tensor_scalar(kind1[:, NR:NR + 1], C, 0.0, None, ALU.is_equal))
            step(dve.tensor_scalar(kind1[:, TSR:TSR + 1], C, 1.0, None, ALU.is_equal))
            step(dve.tensor_reduce(sc[:, 4:5], kind1[:, 0:OTHER], AX.X, ALU.add))
            dve.tensor_scalar(kind1[:, OTHER:KINDS], sc[:, 4:5], -1.0, 1.0, ALU.mult, ALU.add).then_inc(s_kinds, 1)
            step(dve.tensor_scalar(LO, D, 0.0, None, ALU.is_lt))
            step(dve.tensor_scalar(HI, D, float(E), None, ALU.is_ge))
            step(dve.tensor_scalar(sc[:, 5:6], D, 0.0, float(E), ALU.max, ALU.min))
            step(dve.scalar_tensor_tensor(out=sc[:, 6:7], in0=LO, scalar=float(E), in1=sc[:, 5:6],
                                          op0=ALU.mult, op1=ALU.add))
            step(dve.tensor_tensor(sc[:, 7:8], sc[:, 6:7], HI, ALU.add))
            step(dve.tensor_scalar(val3[:, 2:3], sc[:, 7:8], float(H), None, ALU.mult))
            step(dve.tensor_copy(val3[:, 0:1], seq_no[:, :]))
            step(dve.tensor_scalar(val3[:, 1:2], seq_no[:, :], float(-NO_STORE), None, ALU.add))
            dve.wait_ge(s_rank, 2)
            step(dve.tensor_scalar(nslot_i[:, :], H1[:, 0, 0:KINDS], float(G - 1), None, ALU.add))
            step(dve.tensor_scalar(nslot_s[:, :], nslot_i[:, :], G.bit_length() - 1, None, ALU.arith_shift_right))
            step(dve.tensor_copy(sc[:, 8:8 + KINDS], nslot_s[:, :]))
            step(dve.memset(start[:, 0:1], 0.0))
            for k in range(KINDS):
                step(dve.tensor_tensor(start[:, k + 1:k + 2], start[:, k:k + 1], sc[:, 8 + k:9 + k], ALU.add))
            step(dve.tensor_copy(BND[:, :], start[0:1, 1:KINDS + 1]))
            step(dve.scalar_tensor_tensor(out=sc[:, 16:16 + KINDS], in0=start[:, 0:KINDS], scalar=float(G),
                                          in1=H0[:, 0, 0:KINDS], op0=ALU.mult, op1=ALU.add))
            step(dve.tensor_tensor(sc[:, 20:20 + KINDS], sc[:, 16:16 + KINDS], kind1[:, :], ALU.mult))
            step(dve.tensor_reduce(sc[:, 24:25], sc[:, 20:20 + KINDS], AX.X, ALU.add))
            dve.tensor_scalar(place[:, :], pos_no[:, :], sc[:, 24:25], None, ALU.is_equal).then_inc(s_placed, 1)
            dve.wait_ge(s_ids_ps, 1)
            by_pos = H2[0:1, :, :].rearrange("o a n -> o (a n)")
            step(dve.tensor_copy(IDS[:, 0, 0:POS], by_pos[:, 0:POS]))
            step(dve.tensor_scalar(IDS[:, 1, 0:POS], by_pos[:, POS:2 * POS], float(NO_STORE), None, ALU.add))
            dve.tensor_copy(IDS[:, 2, 0:POS], by_pos[:, 2 * POS:3 * POS]).then_inc(s_tables, 1)

            dve.wait_ge(s_e_in, 96)
            dve.wait_ge(s_row_in, 32)
            for c in range(KC):
                for d in range(2):
                    dve.tensor_copy(D0[:, c, d, :], DT[:, c, :])
                    step(dve.tensor_scalar(DG[:, c, d, :], DT[:, c, :], COL[:, COL_G1 + c:COL_G1 + c + 1], None,
                                           ALU.mult))
            step(dve.tensor_tensor(BE[0:A, 0:E], EB[:, :], EM[:, :], ALU.add))
            step(dve.tensor_copy(BE[0:A, E:E + 1], EM[:, 0:1]))
            step(dve.tensor_copy(BE[0:A, E + 1:E + 2], EM[:, E - 1:E]))
            step(dve.memset(BE[A:A + 1, :], 1.0))
            for e in (E, E + 1):
                for d in range(2):
                    last = dve.tensor_copy(EXP[:, e, d, :], ident[0:A, 0:A])
            last.then_inc(s_weights, 1)
            step(dve.memset(S[:, :, :, :].bitcast(F32), 0.0))
            step(dve.memset(X2[:, :, :, :].bitcast(F32), 0.0))
            step(dve.memset(X2[A:A + 2, :, 0:3:2, :].bitcast(F32), 1.0))
            dve.wait_ge(s_bias_ps, 1)
            step(dve.tensor_tensor(BD[:, :], ZP[0][:, 0:1], COL[:, COL_DOWN_B:COL_DOWN_B + 1], ALU.add))
            dve.wait_ge(s_const_ps, 1)
            step(dve.tensor_copy(CH[:, :], ZP[1][0:TE, 0:H]))
            dve.tensor_tensor(CL[:, :], ZP[1][0:TE, 0:H], CH[:, :].bitcast(F32), ALU.subtract).then_inc(s_ct, 1)
            for j in range(TE // 2):
                bank = (TP, UP)[j % 2]
                at = slice(2 * H * j, 2 * H * (j + 1))
                dve.wait_ge(s_fold_hi, j + 1)
                dve.tensor_tensor(T2[0:A, at], bank[0:A, :, :].rearrange("p a n -> p (a n)"),
                                  T1[0:A, at].bitcast(F32), ALU.subtract).then_inc(s_fold_lo, 1)
            dve.sem_inc(s_prep_done, 1)
            dve.sem_inc(z_free, 1)
            dve.sem_inc(z2_free, 1)

            n_slots = bounds(dve)[OTHER]

            def statistics(n, tile, slot, p, tile_ready):
                for t in range(TT):
                    tile_ready(t)
                    dve.bn_stats(ST[n][p][:, t, :], tile[:, t, :]).then_inc(stat[n], 1)
                dve.wait_ge(stat[n], 2 * TT * slot + TT)
                dve.sem_inc(stats_seen, 1)
                for t in range(TT):
                    dve.bn_aggr(MV[n][p][:, t, :], ST[n][p][:, t, :]).then_inc(stat[n], 1)
                dve.wait_ge(stat[n], 2 * TT * slot + 2 * TT)
                dve.tensor_scalar(VE[n][p][:, :], MV[n][p][:, :, 1], EPS, None, ALU.add).then_inc(var[n], 1)

            def minus_mean(n, slot, p):
                dve.wait_ge(rstd[n], slot + 1)
                dve.scalar_tensor_tensor(out=NM[n][p][:, :], in0=MV[n][p][:, :, 0], scalar=-1.0, in1=RS[n][p][:, :],
                                         op0=ALU.mult, op1=ALU.mult).then_inc(nmr[n], 1)

            def both(row):
                return ROW[:, row, :].unsqueeze(1).to_broadcast([P, TT, H])

            for g, i, p, where in steps(dve):
                q = 1 - p
                for _ in on_slot(dve, g, 2, where, n_slots):
                    dve.wait_ge(u_ps, g - 1)
                    dve.wait_ge(y_done, g - 1)
                    dve.tensor_tensor(Z2[p][:, :, :], UP[:, :, :], Y[p][:, :, :], ALU.add).then_inc(z2_free, 1)
                    dve.wait_ge(z2_free, g)
                    statistics(1, Z2[p], g - 2, p, lambda t: None)
                for _ in on_slot(dve, g, 0, where, n_slots):
                    dve.wait_ge(xb, g + 1)
                    for t in range(TT):
                        dve.wait_ge(z_ps[t], g + 1)
                        dve.tensor_tensor(Z[p][:, t, :], ZP[t][:, 0:H], X[p][:, t, :],
                                          ALU.add).then_inc((z_made, z_free)[t], 1)
                    statistics(0, Z[p], g, p, lambda t: dve.wait_ge((z_made, z_free)[t], g + 1 + t))
                for _ in on_slot(dve, g, 2, where, n_slots):
                    minus_mean(1, g - 2, p)
                for _ in on_slot(dve, g, 1, where, n_slots):
                    dve.wait_ge(g_act, g)
                    lo = pair_cols(S)[A:P]
                    dve.tensor_tensor(lo, GF[A:P, :].rearrange("p (a b t) -> p a b t", a=TT, b=2),
                                      lo.bitcast(F32), ALU.subtract)
                    dve.tensor_copy(pair_cols(X2)[0:A], pair_cols(S)[0:A].bitcast(F32)).then_inc(s_made, 1)
                for _ in on_slot(dve, g, 0, where, n_slots):
                    minus_mean(0, g, p)
                for _ in on_slot(dve, g, 2, where, n_slots):
                    dve.wait_ge(n2_act, g - 1)
                    dve.wait_ge(out_free, g - 1)
                    dve.tensor_tensor(O[p][:, :, :], N2[p][:, :, :], both(ROW_G2), ALU.mult).then_inc(o_mul, 1)
                    dve.wait_ge(o_mul, g - 1)
                    dve.tensor_tensor(O[p][:, :, :], O[p][:, :, :], both(ROW_BETA2), ALU.add).then_inc(o_made, 1)

        @block.scalar
        def _(act):
            for j in range(TE // 2):
                bank = (TP, UP)[j % 2]
                act.wait_ge(s_fold, j + 1)
                act.copy(T1[:, 2 * H * j:2 * H * (j + 1)],
                         bank[:, :, :].rearrange("p a n -> p (a n)")).then_inc(s_fold_hi, 1)
            act.wait_ge(s_ct, 1)
            act.dma_start(T2[A:A + 1, :].bitcast(F32), CH[:, :].bitcast(F32)).then_inc(s_ct_in, 16)
            act.dma_start(T2[A + 1:A + 2, :].bitcast(F32), CL[:, :].bitcast(F32)).then_inc(s_ct_in, 16)
            act.wait_ge(s_prep_done, 1)
            b_sr, b_nr, b_tsr, n_slots = bounds(act)

            def gelu(dst, src, col):
                return act.activation(dst, src, ACT.Gelu, bias=COL[:, col:col + 1])

            def normalise(n, dst, src, slot, p, ready):
                act.wait_ge(nmr[n], slot + 1)
                for t in range(TT):
                    ins = act.activation(dst[:, t, :], src[:, t, :], ACT.Identity, bias=NM[n][p][:, t:t + 1],
                                         scale=RS[n][p][:, t:t + 1])
                ins.then_inc(ready, 1)

            for g, i, p, where in steps(act):
                for _ in on_slot(act, g, 0, where, n_slots):
                    with act.If(g < b_sr):
                        for bank, ready, made, at in ((H0, h0_ps, h0_act, 0), (H1, h1_ps, h1_act, 2)):
                            act.wait_ge(ready, g + 1)
                            gelu(h1[:, at, :], bank[:, 0, :], COL_B1_SR + at)
                            gelu(h1[:, at + 1, :], bank[:, 1, :], COL_B1_SR + at + 1).then_inc(made, 1)
                    with act.Else():
                        def two_layer(col):
                            act.wait_ge(h0_ps, g + 1)
                            gelu(h2[:, 0, :], H0[:, 0, :], col).then_inc(h0_act, 1)
                            act.wait_ge(h1_ps, g + 1)
                            gelu(h2[:, 1, :], H1[:, 0, :], col + 1).then_inc(h1_act, 1)

                        with act.If(g < b_nr):
                            two_layer(COL_B1_NR)
                        with act.Else():
                            two_layer(COL_B1_TSR)
                for _ in on_slot(act, g, 1, where, n_slots):
                    act.wait_ge(t_ps, g)
                    act.copy(YT[:, :, :], TP[:, :, :]).then_inc(yt_act, 1)
                for _ in on_slot(act, g, 0, where, n_slots):
                    with act.If(g < b_sr):
                        act.wait_ge(h2_ps, g + 1)
                        gelu(h2[:, 0, :], H2[:, 0, :], COL_B2_SR)
                        gelu(h2[:, 1, :], H2[:, 1, :], COL_B2_SR + 1).then_inc(h2_act, 1)
                for _ in on_slot(act, g, 2, where, n_slots):
                    normalise(1, N2[p], Z2[p], g - 2, p, n2_act)
                for _ in on_slot(act, g, 1, where, n_slots):
                    act.wait_ge(d_ps, g)
                    src = DP[:, 0:N].rearrange("p (a b t) -> p a b t", a=TT, b=2)
                    act.activation(pair_cols(S), src, ACT.Gelu, bias=BD[:, :])
                    act.activation(GF[A:P, :], DP[A:P, 0:N], ACT.Gelu, bias=BD[A:P, :]).then_inc(g_act, 1)
                for _ in on_slot(act, g, 0, where, n_slots):
                    normalise(0, ZN, Z[p], g, p, zn_act)

        @block.tensor
        def _(pe):
            pe.wait_ge(s_const, 3)
            pe.wait_ge(s_kinds, 1)
            pe.matmul(H0[:, 0, 0:KINDS], before[:, :], kind1[:, :], start=True, stop=True).then_inc(s_rank, 1)
            pe.matmul(H1[:, 0, 0:KINDS], ones[:, :], kind1[:, :], start=True, stop=True).then_inc(s_rank, 1)
            pe.wait_ge(s_placed, 1)
            by_pos = H2[0:1, :, :].rearrange("o a n -> o (a n)")
            for r in range(3):
                ins = pe.matmul(by_pos[:, r * POS:(r + 1) * POS], val3[:, r:r + 1], place[:, :],
                                start=True, stop=True)
            ins.then_inc(s_ids_ps, 1)
            pe.wait_ge(s_weights, 1)
            for c in range(KC):
                ins = pe.matmul(ZP[0][:, 0:1], D0[:, c, :, :].rearrange("p a n -> p (a n)"),
                                COL[:, COL_BETA1 + c:COL_BETA1 + c + 1], start=(c == 0), stop=(c == KC - 1))
            ins.then_inc(s_bias_ps, 1)
            pe.matmul(ZP[1][0:TE, 0:H], BE[:, :], UPB[:, :], start=True, stop=True).then_inc(s_const_ps, 1)
            for j in range(TE // 2):
                bank = (TP, UP)[j % 2]
                if j >= 2:
                    pe.wait_ge(s_fold_lo, j - 1)
                for e in range(2):
                    ins = pe.matmul(bank[:, e, :], EXP[:, 2 * j + e, :, :].rearrange("p a n -> p (a n)"),
                                    UPB[0:A, :], start=True, stop=True)
                ins.then_inc(s_fold, 1)
            pe.wait_ge(s_w_in, 7 * 16)
            pe.wait_ge(s_prep_done, 1)
            pe.wait_ge(s_ct_in, 32)
            b_sr, b_nr, b_tsr, n_slots = bounds(pe)

            def first_layer(w, g, p, i, per_bank):
                pe.wait_ge(ld_xf[p], 16 * G * (i + 1))
                for m in range(2 * per_bank):
                    bank, ready = ((H0, h0_ps), (H1, h1_ps))[m // per_bank]
                    for c in range(KC):
                        ins = pe.matmul(bank[:, m % per_bank, :], w[:, c, m * P:(m + 1) * P], XF[p][:, :, c, :],
                                        start=(c == 0), stop=(c == KC - 1))
                    if m % per_bank == per_bank - 1:
                        ins.then_inc(ready, 1)

            def last_layer(h, w, g):
                pe.wait_ge(z_free, g + 1)
                for t in range(TT):
                    for c in range(KC):
                        ins = pe.matmul(ZP[t][:, 0:H], h[:, c, t * P:(t + 1) * P], w[:, c, :],
                                        start=(c == 0), stop=(c == KC - 1))
                    ins.then_inc(z_ps[t], 1)

            for g, i, p, where in steps(pe):
                for _ in on_slot(pe, g, 0, where, n_slots):
                    with pe.If(g < b_sr):
                        first_layer(W1[SR], g, p, i, 2)
                    with pe.Else():
                        with pe.If(g < b_nr):
                            first_layer(W1[NR], g, p, i, 1)
                        with pe.Else():
                            with pe.If(g < b_tsr):
                                first_layer(W1[TSR], g, p, i, 1)
                            with pe.Else():
                                pe.matmul(H0[:, 0, :], zeros[:, 0:P], zeros[:, 0:N], start=True,
                                          stop=True).then_inc(h0_ps, 1)
                                pe.matmul(H1[:, 0, :], zeros[:, 0:P], zeros[:, 0:N], start=True,
                                          stop=True).then_inc(h1_ps, 1)
                for _ in on_slot(pe, g, 2, where, n_slots):
                    at = four(pe, 2, g - 2, (TE - 1) * H)
                    pe.wait_ge(s_made, g - 1)
                    pe.wait_ge(z2_free, g - 1)
                    for t in range(TT):
                        for d in range(2):
                            cols_s = S[:, t, :, :].rearrange("p a n -> p (a n)")[:, d * T:d * T + P]
                            cols_x = X2[:, t, :, :].rearrange("p a n -> p (a n)")[:, d * T:d * T + P]
                            pe.matmul(UP[:, t, :], cols_s, T1[:, bass.ds(at[2 * t + d], H)],
                                      start=(d == 0), stop=False)
                            ins = pe.matmul(UP[:, t, :], cols_x, T2[:, bass.ds(at[2 * t + d], H)],
                                            start=False, stop=(d == 1))
                    ins.then_inc(u_ps, 1)
                for _ in on_slot(pe, g, 1, where, n_slots):
                    pe.wait_ge(zn_act, g)
                    for c in range(KC):
                        for t in range(TT):
                            ins = pe.transpose(TP[:, c, t * P:(t + 1) * P], ZN[:, t, c * P:(c + 1) * P],
                                               ident[:, :])
                    ins.then_inc(t_ps, 1)
                for _ in on_slot(pe, g, 0, where, n_slots):
                    with pe.If(g < b_sr):
                        for m in range(KC):
                            for c in range(2 * KC):
                                if m == 0 and c % 2 == 0:
                                    pe.wait_ge((h0_act, h1_act)[c // 2], g + 1)
                                ins = pe.matmul(H2[:, m, :], W2[SR][:, c, m * P:(m + 1) * P], h1[:, c, :],
                                                start=(c == 0), stop=(c == 2 * KC - 1))
                        ins.then_inc(h2_ps, 1)
                    with pe.Else():
                        with pe.If(g < b_nr):
                            pe.wait_ge(h0_act, g + 1)
                            pe.wait_ge(h1_act, g + 1)
                            last_layer(h2, W2[NR], g)
                        with pe.Else():
                            with pe.If(g < b_tsr):
                                pe.wait_ge(h0_act, g + 1)
                                pe.wait_ge(h1_act, g + 1)
                                last_layer(h2, W2[TSR], g)
                            with pe.Else():
                                pe.wait_ge(h0_act, g + 1)
                                pe.wait_ge(h1_act, g + 1)
                                pe.wait_ge(z_free, g + 1)
                                for t in range(TT):
                                    pe.matmul(ZP[t][:, 0:H], zeros[:, 0:P], zeros[:, 0:H], start=True,
                                              stop=True).then_inc(z_ps[t], 1)
                for _ in on_slot(pe, g, 1, where, n_slots):
                    pe.wait_ge(yt_act, g)
                    for c in range(KC):
                        ins = pe.matmul(DP[:, 0:N], DG[:, c, :, :].rearrange("p a n -> p (a n)"), YT[:, c, :],
                                        start=(c == 0), stop=(c == KC - 1))
                    ins.then_inc(d_ps, 1)
                for _ in on_slot(pe, g, 0, where, n_slots):
                    with pe.If(g < b_sr):
                        pe.wait_ge(h2_act, g + 1)
                        last_layer(h2, W3, g)


def kernel(**inputs):
    import numpy as np
    import concourse.bacc as bacc
    from concourse.bass_utils import run_bass_kernel_spmd as run

    v = {k: np.ascontiguousarray(a) for k, a in inputs.items()}
    x = v["x"]
    B, T, H = x.shape
    KC = H // P

    def halves(name):
        return v[name].reshape(-1, P).T

    down_b = v["L1_cond_down_b"]
    data = {
        "x_tok": x,
        "x_feat": x.transpose(0, 2, 1).reshape(B, KC, P, T).transpose(0, 2, 1, 3),
        "cond": v["itok_B_0_2"].reshape(B, 1),
        "dom": v["itok_B_0_15"].reshape(B, 1),
        "w1_nr": v["L0_cond_w1_nr"], "w2_nr": v["L0_cond_w2_nr"],
        "w1_tsr": v["L0_cond_w1_tsr"], "w2_tsr": v["L0_cond_w2_tsr"],
        "w1_sr": v["L0_cond_w1_sr"], "w2_sr": v["L0_cond_w2_sr"], "w3_sr": v["L0_cond_w3_sr"],
        "cols": np.concatenate([halves("L0_cond_b1_nr"), halves("L0_cond_b1_tsr"), halves("L0_cond_b1_sr"),
                                halves("L0_cond_b2_sr"), halves("L0_cond_gamma"), halves("L0_cond_beta"),
                                np.concatenate([down_b, down_b]).reshape(P, 1)], axis=1),
        "rows": np.stack([v["L0_cond_b3_sr"], v["L0_cond_b2_nr"], v["L0_cond_b2_tsr"], v["L0_cond_gamma"],
                          v["L1_cond_ln_gamma"], v["L0_cond_beta"], v["L1_cond_ln_beta"]]),
        "down_t": v["L1_cond_down_W"].T.reshape(KC, P, -1).transpose(1, 0, 2),
        "up_b1": np.concatenate([v["L1_cond_up_W"].T, v["L1_cond_up_b"][None]], axis=0),
        "expert_t": v["L1_cond_expert_W"].transpose(1, 0, 2),
        "expert_b_t": v["L1_cond_expert_b"].T,
        "emb_t": v["L1_cond_domain_emb"].T,
    }
    nc = bacc.Bacc("TRN2", target_bir_lowering=False, num_devices=1)
    arrays, args = {}, []
    for name, a in data.items():
        a = np.ascontiguousarray(a)
        arrays[f"in_{name}"] = a
        args.append(nc.dram_tensor(f"in_{name}", a.shape, mybir.dt.from_np(a.dtype), kind="ExternalInput").ap())
    args.append(nc.dram_tensor("out_0", (B, T, H), F32, kind="ExternalOutput").ap())
    conditioned_layers(nc, *args)
    r = run(nc, [arrays], core_ids=[0])
    return r.results[0]["out_0"]
```

```python
from contextlib import ExitStack

import concourse.bass as bass
from concourse import mybir

F32 = mybir.dt.float32
F32R = mybir.dt.float32r
I32 = mybir.dt.int32
ALU = mybir.AluOpType
ACT = mybir.ActivationFunctionType
AX = mybir.AxisListType

P = 128
EPS = 1e-5

SR, NR, TSR, OTHER = range(4)
KINDS = 4
COL_B2_SR, COL_B1_NR, COL_B1_TSR, COL_B1_SR, COL_G1, COL_BETA1, COL_DOWN_B, COLS = 0, 2, 4, 6, 10, 12, 14, 15


def conditioned_layers(nc, x_feat, cond, dom, w1_nr, w2_nr, w1_tsr, w2_tsr, w1_sr, w2_sr, w3_sr,
                       cols, last_b, gain2, down_t, up_b1, expert_t, expert_b_t, emb_t, out):
    B, _, T, KC = x_feat.shape
    H = KC * P
    A = down_t.shape[-1]
    E = expert_t.shape[1]
    TE = E + 2
    G = 4
    N = G * T
    TT = N // P
    S_MIN = B // G
    S_MAX = S_MIN + KINDS - 1
    POS = (S_MAX + 1) * G
    WIDTH = POS + 6 * G
    assert B == P and 2 * T == P and 2 * A == P and TT == 2 and KC == 2
    assert out.shape[0] == B + KINDS * (G - 1)

    with ExitStack() as ctx:
        def sb(name, shape, dt=F32):
            return ctx.enter_context(nc.sbuf_tensor(name, shape, dt))

        def ps(name, shape):
            return ctx.enter_context(nc.psum_tensor(name, shape, F32))

        def sem(name):
            return ctx.enter_context(nc.semaphore(name))

        W_DRAM = {"w1_sr": w1_sr, "w2_sr": w2_sr, "w3_sr": w3_sr, "w1_nr": w1_nr, "w2_nr": w2_nr,
                  "w1_tsr": w1_tsr, "w2_tsr": w2_tsr}
        LAST = {"w3_sr": SR, "w2_nr": NR, "w2_tsr": TSR}
        W, WH, WL = {}, {}, {}
        for name, w in W_DRAM.items():
            if name in LAST:
                continue
            shape = [P, w.shape[0] // P, w.shape[1]]
            W[name] = sb(name + "_sb", shape)[:, :, :]
            WH[name] = sb(name + "_hi", shape, F32R)[:, :, :]
            WL[name] = sb(name + "_lo", shape, F32R)[:, :, :]
        last_f = sb("last_sb", [P, KINDS, KC, H])
        last_hi = sb("last_hi", [P, KINDS * KC * H], F32R)
        last_lo = sb("last_lo", [P, KINDS * KC * H], F32R)
        for name, kind in LAST.items():
            at = slice(kind * KC * H, (kind + 1) * KC * H)
            W[name] = last_f[:, kind, :, :]
            WH[name] = last_hi[:, at].rearrange("p (c n) -> p c n", c=KC)
            WL[name] = last_lo[:, at].rearrange("p (c n) -> p c n", c=KC)
        COL = sb("col_sb", [P, COLS])
        LB = sb("last_b_sb", [1, KINDS, TT, H])
        LBH = sb("last_b_hi", [2, KINDS * TT * H], F32R)
        LBL = sb("last_b_lo", [1, KINDS * TT * H], F32R)
        G2 = sb("gain2_sb", [P, 2, H])
        DD = sb("down_dup", [P, KC, 2, A])
        UPB = sb("up_b_sb", [A + 1, H])
        EXP = sb("expert_sb", [A, TE, 2, A])
        EB = sb("expert_b_sb", [A, E])
        EM = sb("emb_sb", [A, E])
        CONDI = sb("cond_i", [P, 1], I32)
        DOMI = sb("dom_i", [P, 1], I32)
        ident = sb("ident", [P, P])
        before = sb("before", [P, P])
        ones = sb("ones", [P, P])
        ones2 = sb("ones2", [2, P], F32R)
        seq_no = sb("seq_no", [P, 1])
        pos_no = sb("pos_no", [P, POS])
        sc = sb("sort_scratch", [P, 40])
        kind1 = sb("kind_onehot", [P, KINDS])
        start = sb("kind_start", [P, KINDS + 1])
        nslot_i = sb("kind_slots_i", [P, KINDS], I32)
        nslot_s = sb("kind_slots_s", [P, KINDS], I32)
        table_at = sb("table_at", [P, 1])
        kind_no = sb("kind_no", [P, 1])
        place = sb("place", [P, POS])
        below = sb("below", [P, POS])
        pad = sb("pad_scratch", [1, 4, POS])
        IDS = sb("ids", [1, 4, WIDTH], I32)
        BND = sb("bounds", [1, KINDS], I32)
        BE = sb("expert_const", [A + 1, TE])
        CH = sb("const_hi", [TE, H], F32R)
        CL = sb("const_lo", [TE, H], F32R)
        T1 = sb("table_hi", [P, TE * H], F32R)
        T2 = sb("table_lo", [A + 2, TE * H], F32R)
        mhalf = sb("minus_half", [P, TT])
        XF = [sb(f"x{p}", [P, G, T, KC]) for p in range(2)]
        XH = [sb(f"x_hi{p}", [P, G, T, KC], F32R) for p in range(2)]
        XL = [sb(f"x_lo{p}", [P, G, T, KC], F32R) for p in range(2)]
        h1 = sb("h1", [P, 2 * KC, N])
        h1h = sb("h1_hi", [P, 2 * KC, N], F32R)
        h1l = sb("h1_lo", [P, 2 * KC, N], F32R)
        h2 = sb("h2", [P, KC, N])
        h2h = sb("h2_hi", [P, KC, N], F32R)
        h2l = sb("h2_lo", [P, KC, N], F32R)
        ZN = sb("zn", [P, TT, H])
        YT = [sb(f"yt{p}", [P, KC, N]) for p in range(2)]
        GF = [sb(f"gelu_f{p}", [P, N]) for p in range(2)]
        S = [sb(f"stack{p}", [P, TT, 3, T], F32R) for p in range(2)]
        X2 = [sb(f"stack_hi{p}", [A + 2, TT, 3, T], F32R) for p in range(2)]
        N2 = [sb(f"n{p}", [P, TT, H]) for p in range(2)]
        O = [sb(f"o{p}", [P, TT, H]) for p in range(2)]
        ST = [[sb(f"st{n}{p}", [P, TT, 6]) for p in range(2)] for n in range(2)]
        MV = [[sb(f"mv{n}{p}", [P, TT, 2]) for p in range(2)] for n in range(2)]
        VE = [[sb(f"ve{n}{p}", [P, TT]) for p in range(2)] for n in range(2)]
        RS = [[sb(f"rs{n}{p}", [P, TT]) for p in range(2)] for n in range(2)]
        NM = [[sb(f"nm{n}{p}", [P, TT]) for p in range(2)] for n in range(2)]

        H0 = ps("ps_h0", [P, 2, N])
        H1 = ps("ps_h1", [P, 2, N])
        ZP = [ps(f"ps_z{p}", [P, TT, H]) for p in range(2)]
        TP = ps("ps_t", [P, KC, N])
        DP = ps("ps_d", [P, 2 * N])
        UP = [ps(f"ps_u{p}", [P, TT, H]) for p in range(2)]

        s_ids_in = sem("s_ids_in")
        s_col_in = sem("s_col_in")
        s_lb_in = sem("s_lb_in")
        s_g2_in = sem("s_g2_in")
        s_w_in = {n: sem("in_" + n) for n in W}
        s_wh = {n: sem("hi_" + n) for n in W}
        s_wl = {n: sem("lo_" + n) for n in W}
        s_e_in = sem("s_e_in")
        s_const = sem("s_const")
        s_prep = sem("s_prep")
        s_kinds = sem("s_kinds")
        s_zero_last = sem("s_zero_last")
        s_placed = sem("s_placed")
        s_weights = sem("s_weights")
        s_rank = sem("s_rank")
        s_ids_ps = sem("s_ids_ps")
        s_load_ids = sem("s_load_ids")
        s_ids = sem("s_ids")
        s_const_ps = sem("s_const_ps")
        s_ct = sem("s_ct")
        s_ct_in = sem("s_ct_in")
        s_lb = sem("s_lb")
        s_lb_low = sem("s_lb_low")
        s_fold = sem("s_fold")
        s_fold_hi = sem("s_fold_hi")
        s_fold_lo = sem("s_fold_lo")
        s_stack = sem("s_stack")
        ld_x = [sem(f"ld_x{p}") for p in range(2)]
        st_out = [sem(f"st_out{p}") for p in range(2)]
        out_free = sem("out_free")
        x_hi = sem("x_hi")
        x_lo = sem("x_lo")
        x_used = sem("x_used")
        h0_ps = sem("h0_ps")
        h1_ps = sem("h1_ps")
        h2_ps = sem("h2_ps")
        h0_hi = sem("h0_hi")
        h1_hi = sem("h1_hi")
        h2_hi = sem("h2_hi")
        h0_full = sem("h0_full")
        h1_full = sem("h1_full")
        h2_full = sem("h2_full")
        h0_lo = sem("h0_lo")
        h1_lo = sem("h1_lo")
        h2_lo = sem("h2_lo")
        z_ps = sem("z_ps")
        stat = [sem("stat1"), sem("stat2")]
        stats_seen = sem("stats_seen")
        var = [sem("var1"), sem("var2")]
        rstd = [sem("rstd1"), sem("rstd2")]
        nmr = [sem("nmr1"), sem("nmr2")]
        zn_act = sem("zn_act")
        t_ps = sem("t_ps")
        yt_act = sem("yt_act")
        d_ps = sem("d_ps")
        g_act = sem("g_act")
        s_made = sem("s_made")
        u_ps = sem("u_ps")
        n2_act = sem("n2_act")
        o_mul = sem("o_mul")
        o_made = sem("o_made")

        HEAD, MAIN, TAIL = "head", "main", "tail"
        HEAD_STEPS = 4
        TAIL_START = S_MIN - S_MIN % 2 - 2
        LAST_STEP = S_MAX + 4

        def steps(eng):
            for g in range(-1, HEAD_STEPS):
                yield g, g // 2, g % 2, HEAD
            for first, last, where in ((HEAD_STEPS, TAIL_START, MAIN), (TAIL_START, LAST_STEP + 1, TAIL)):
                with eng.Fori(first // 2, last // 2) as i:
                    for p in range(2):
                        yield 2 * i + p, i, p, where

        def on_slot(eng, g, lag, where, n_slots):
            if where == TAIL:
                with eng.If(g < n_slots + lag):
                    yield g - lag
            elif where == MAIN or g >= lag:
                yield g - lag

        def bounds(eng):
            eng.wait_ge(s_load_ids, 1)
            _, v = nc.values_load_multi_w_load_instructions(
                BND[0:1, 0:KINDS], engines=[eng.engine], min_val=0, max_val=S_MAX,
                skip_runtime_bounds_check_because="sums of counts that add up to the number of sequences")
            return v

        def four(eng, row, slot, top):
            _, v = nc.values_load_multi_w_load_instructions(
                IDS[0:1, row, bass.ds(slot * G, G)], engines=[eng.engine], min_val=0, max_val=top,
                skip_runtime_bounds_check_because="the entries are worked out from one-hot sums")
            return v

        def kind_of(eng, slot):
            _, v = nc.values_load_multi_w_load_instructions(
                IDS[0:1, 3, bass.ds(slot * G, 1)], engines=[eng.engine], min_val=0, max_val=OTHER,
                skip_runtime_bounds_check_because="the entries are worked out from one-hot sums")
            return v[0]

        def pair_cols(tile):
            return tile[:, :, 0:3:2, :]

        def flat(ap):
            return ap.rearrange("p a n -> p (a n)")

        block = ctx.enter_context(nc.Block())

        @block.sync
        def _(sp):
            sp.dma_start(CONDI[:, :], cond).then_inc(s_ids_in, 16)
            sp.dma_start(DOMI[:, :], dom).then_inc(s_ids_in, 16)
            for name in W:
                sp.dma_start(W[name],
                             W_DRAM[name].rearrange("(c p) n -> p c n", p=P)).then_inc(s_w_in[name], 16)

            def load(slot, p, tile_free):
                ids = four(sp, 0, slot, B - 1)
                tile_free()
                for k in range(G):
                    src = x_feat[bass.ds(ids[k], 1), :, :, :].rearrange("a p t c -> (a p) t c")
                    sp.dma_start(XF[p][:, k, :, :], src).then_inc(ld_x[p], 16)

            n_slots = bounds(sp)[OTHER]
            for p in range(2):
                load(p, p, lambda: None)
            sp.sem_inc(out_free, 2)
            sp.wait_ge(s_ids, 1)
            for g, i, p, where in steps(sp):
                if not (where == HEAD and g < 0):
                    for slot in on_slot(sp, g, -2, where, n_slots):
                        load(slot, p, lambda: sp.wait_ge(x_used, g + 1))
                for slot in on_slot(sp, g, 4, where, n_slots):
                    sp.wait_ge(st_out[p], 16 * G * (i - 1))
                    sp.sem_inc(out_free, 1)
                for slot in on_slot(sp, g, 3, where, n_slots):
                    q = 1 - p
                    ids = four(sp, 1, slot, out.shape[0] - 1)
                    sp.wait_ge(o_made, slot + 1)
                    for k in range(G):
                        sp.dma_start(out[bass.ds(ids[k], 1), :, :].rearrange("a t n -> (a t) n"),
                                     O[q][T * (k % 2):T * (k % 2) + T, k // 2, :]).then_inc(st_out[q], 16)

        @block.gpsimd
        def _(pool):
            pool.memset(ones[:, :], 1.0)
            pool.memset(ident[:, :], 0.0).then_inc(s_const, 1)
            pool.iota(seq_no[:, :], pattern=[[0, 1]], base=0, channel_multiplier=1,
                      allow_small_or_imprecise_dtypes=True)
            pool.iota(pos_no[:, :], pattern=[[1, POS]], base=0, channel_multiplier=0,
                      allow_small_or_imprecise_dtypes=True).then_inc(s_const, 1)
            pool.wait_ge(s_const, 2)
            pool.affine_select(out=before[:, :], in_=ones[:, :], compare_op=ALU.is_gt, fill=0.0, base=0,
                               pattern=[[1, P]], channel_multiplier=-1)
            pool.affine_select(out=ident[:, :], in_=ident[:, :], compare_op=ALU.not_equal, fill=1.0, base=0,
                               pattern=[[-1, P]], channel_multiplier=1)
            pool.memset(mhalf[:, :], -0.5).then_inc(s_const, 1)

            def low_half(name):
                pool.wait_ge(s_wh[name], 1)
                pool.tensor_tensor(WL[name], W[name], WH[name].bitcast(F32),
                                   ALU.subtract).then_inc(s_wl[name], 1)

            low_half("w1_sr")

            n_slots_all = bounds(pool)
            b_sr, n_slots = n_slots_all[SR], n_slots_all[OTHER]
            for name in ("w2_sr", "w3_sr", "w1_nr", "w2_nr", "w1_tsr", "w2_tsr"):
                low_half(name)

            def low(dst, full, high, made, ready, g):
                pool.wait_ge(made, g + 1)
                pool.tensor_tensor(dst, full, high.bitcast(F32), ALU.subtract).then_inc(ready, 1)

            def power(n, slot, p):
                pool.wait_ge(var[n], slot + 1)
                pool.tensor_tensor(RS[n][p][:, :], VE[n][p][:, :], mhalf[:, :], ALU.pow).then_inc(rstd[n], 1)

            for g, i, p, where in steps(pool):
                q = 1 - p

                def last_power():
                    for slot in on_slot(pool, g, 3, where, n_slots):
                        power(1, slot, q)

                with pool.If(g < b_sr):
                    for slot in on_slot(pool, g, 0, where, n_slots):
                        low(h1l[:, 0:2, :], h1[:, 0:2, :], h1h[:, 0:2, :], h0_full, h0_lo, g)
                        low(h1l[:, 2:4, :], h1[:, 2:4, :], h1h[:, 2:4, :], h1_full, h1_lo, g)
                        last_power()
                        low(h2l[:, :, :], h2[:, :, :], h2h[:, :, :], h2_full, h2_lo, g)
                        power(0, slot, p)
                with pool.Else():
                    for slot in on_slot(pool, g, 0, where, n_slots):
                        low(h2l[:, 0, :], h2[:, 0, :], h2h[:, 0, :], h0_full, h0_lo, g)
                        low(h2l[:, 1, :], h2[:, 1, :], h2h[:, 1, :], h1_full, h1_lo, g)
                    last_power()
                    for slot in on_slot(pool, g, 0, where, n_slots):
                        power(0, slot, p)

        @block.vector
        def _(dve):
            done = [0]

            def step(ins):
                done[0] += 1
                ins.then_inc(s_prep, 1)
                dve.wait_ge(s_prep, done[0])

            C, D, LO, HI = sc[:, 0:1], sc[:, 1:2], sc[:, 2:3], sc[:, 3:4]
            for half in (last_hi, last_lo):
                ins = dve.memset(half[:, OTHER * KC * H:].bitcast(F32), 0.0)
            ins.then_inc(s_zero_last, 1)
            dve.memset(start[:, 0:1], 0.0)
            dve.wait_ge(s_ids_in, 32)
            step(dve.tensor_copy(C, CONDI[:, :]))
            dve.tensor_copy(D, DOMI[:, :])
            dve.tensor_scalar(kind1[:, SR:SR + 1], C, 2.0, None, ALU.is_equal)
            dve.tensor_scalar(kind1[:, NR:NR + 1], C, 0.0, None, ALU.is_equal)
            step(dve.tensor_scalar(kind1[:, TSR:TSR + 1], C, 1.0, None, ALU.is_equal))
            step(dve.tensor_reduce(sc[:, 4:5], kind1[:, 0:OTHER], AX.X, ALU.add))
            dve.tensor_scalar(kind1[:, OTHER:KINDS], sc[:, 4:5], -1.0, 1.0, ALU.mult, ALU.add).then_inc(s_kinds, 1)
            dve.tensor_scalar(LO, D, 0.0, None, ALU.is_lt)
            dve.tensor_scalar(HI, D, float(E), None, ALU.is_ge)
            step(dve.tensor_scalar(sc[:, 5:6], D, 0.0, float(E), ALU.max, ALU.min))
            step(dve.scalar_tensor_tensor(out=sc[:, 6:7], in0=LO, scalar=float(E), in1=sc[:, 5:6],
                                          op0=ALU.mult, op1=ALU.add))
            step(dve.tensor_tensor(sc[:, 7:8], sc[:, 6:7], HI, ALU.add))
            dve.scalar_tensor_tensor(out=sc[:, 30:31], in0=kind1[:, TSR:TSR + 1], scalar=2.0,
                                     in1=kind1[:, NR:NR + 1], op0=ALU.mult, op1=ALU.add)
            step(dve.tensor_scalar(table_at[:, :], sc[:, 7:8], float(H), None, ALU.mult))
            step(dve.scalar_tensor_tensor(out=kind_no[:, :], in0=kind1[:, OTHER:KINDS], scalar=float(OTHER),
                                          in1=sc[:, 30:31], op0=ALU.mult, op1=ALU.add))
            dve.wait_ge(s_rank, 2)
            step(dve.tensor_scalar(nslot_i[:, :], H1[:, 0, 0:KINDS], float(G - 1), None, ALU.add))
            step(dve.tensor_scalar(nslot_s[:, :], nslot_i[:, :], G.bit_length() - 1, None, ALU.arith_shift_right))
            step(dve.tensor_copy(sc[:, 8:8 + KINDS], nslot_s[:, :]))
            for k in range(KINDS):
                step(dve.tensor_tensor(start[:, k + 1:k + 2], start[:, k:k + 1], sc[:, 8 + k:9 + k], ALU.add))
            dve.tensor_copy(BND[:, :], start[0:1, 1:KINDS + 1])
            step(dve.scalar_tensor_tensor(out=sc[:, 16:16 + KINDS], in0=start[:, 0:KINDS], scalar=float(G),
                                          in1=H0[:, 0, 0:KINDS], op0=ALU.mult, op1=ALU.add))
            step(dve.tensor_tensor(sc[:, 20:20 + KINDS], sc[:, 16:16 + KINDS], kind1[:, :], ALU.mult))
            step(dve.tensor_reduce(sc[:, 24:25], sc[:, 20:20 + KINDS], AX.X, ALU.add))
            dve.wait_ge(s_const, 3)
            dve.tensor_scalar(place[:, :], pos_no[:, :], sc[:, 24:25], None, ALU.is_equal).then_inc(s_placed, 1)
            dve.tensor_scalar(below[:, :], pos_no[:, :], sc[:, 24:25], None, ALU.is_gt).then_inc(s_placed, 1)
            dve.wait_ge(s_ids_ps, 1)
            dve.tensor_copy(IDS[:, 0, 0:POS], ZP[0][0:1, 0, 0:POS]).then_inc(s_load_ids, 1)
            dve.wait_ge(s_ids_ps, 2)
            step(dve.tensor_scalar(pad[:, 0, :], H1[0:1, 1, 0:POS], -1.0, float(B), ALU.mult, ALU.add))
            step(dve.tensor_tensor(pad[:, 1, :], pad[:, 0, :], pos_no[0:1, :], ALU.add))
            step(dve.tensor_tensor(pad[:, 2, :], DP[0:1, 0:POS], pad[:, 1, :], ALU.mult))
            step(dve.tensor_tensor(pad[:, 3, :], pad[:, 1, :], pad[:, 2, :], ALU.subtract))
            step(dve.tensor_tensor(IDS[:, 1, 0:POS], ZP[0][0:1, 0, 0:POS], pad[:, 3, :], ALU.add))
            dve.tensor_copy(IDS[:, 3, 0:POS], TP[0:1, 1, 0:POS])
            dve.tensor_copy(IDS[:, 2, 0:POS], H0[0:1, 1, 0:POS]).then_inc(s_ids, 1)

            dve.wait_ge(s_e_in, 80)
            dve.tensor_tensor(BE[0:A, 0:E], EB[:, :], EM[:, :], ALU.add)
            dve.tensor_copy(BE[0:A, E:E + 1], EM[:, 0:1])
            dve.tensor_copy(BE[0:A, E + 1:E + 2], EM[:, E - 1:E])
            dve.memset(BE[A:A + 1, :], 1.0)
            for e in (E, E + 1):
                for d in range(2):
                    last = dve.tensor_copy(EXP[:, e, d, :], ident[0:A, 0:A])
            last.then_inc(s_weights, 1)
            dve.wait_ge(s_lb_in, 32)
            dve.memset(ones2[:, :].bitcast(F32), 1.0)
            lb = LB[:, :, :, :].rearrange("p k t n -> p (k t n)")
            step(dve.memset(LB[:, OTHER, :, :], 0.0))
            step(dve.tensor_copy(LBH[0:1, :], lb))
            dve.tensor_tensor(LBL[:, :], lb, LBH[0:1, :].bitcast(F32),
                              ALU.subtract).then_inc(s_lb, 1)
            n_slots = bounds(dve)[OTHER]

            def input_high(slot, i, p):
                dve.wait_ge(ld_x[p], 16 * G * (i + 1))
                dve.tensor_copy(XH[p][:, :, :, :], XF[p][:, :, :, :]).then_inc(x_hi, 1)

            def input_low(slot, p):
                dve.wait_ge(x_hi, slot + 1)
                dve.tensor_tensor(XL[p][:, :, :, :], XF[p][:, :, :, :], XH[p][:, :, :, :].bitcast(F32),
                                  ALU.subtract).then_inc(x_lo, 1)

            input_high(0, 0, 0)
            input_low(0, 0)
            dve.wait_ge(s_const_ps, 1)
            step(dve.tensor_copy(CH[:, :], TP[0:TE, 0, :]))
            dve.tensor_tensor(CL[:, :], TP[0:TE, 0, :], CH[:, :].bitcast(F32), ALU.subtract).then_inc(s_ct, 1)
            for p in range(2):
                step(dve.memset(S[p][:, :, :, :].bitcast(F32), 0.0))
                step(dve.memset(X2[p][:, :, :, :].bitcast(F32), 0.0))
                dve.memset(X2[p][A:A + 2, :, 0:3:2, :].bitcast(F32), 1.0).then_inc(s_stack, 1)
            for j in range(TE // 2):
                bank = UP[j % 2]
                at = slice(2 * H * j, 2 * H * (j + 1))
                dve.wait_ge(s_fold_hi, j + 1)
                dve.tensor_tensor(T2[0:A, at], flat(bank[0:A, :, :]), T1[0:A, at].bitcast(F32),
                                  ALU.subtract).then_inc(s_fold_lo, 1)

            def statistics(n, bank, slot, p):
                for t in range(TT):
                    dve.bn_stats(ST[n][p][:, t, :], bank[:, t, :]).then_inc(stat[n], 1)
                dve.wait_ge(stat[n], 2 * TT * slot + TT)
                dve.sem_inc(stats_seen, 1)
                for t in range(TT):
                    dve.bn_aggr(MV[n][p][:, t, :], ST[n][p][:, t, :]).then_inc(stat[n], 1)
                dve.wait_ge(stat[n], 2 * TT * slot + 2 * TT)
                dve.tensor_scalar(VE[n][p][:, :], MV[n][p][:, :, 1], EPS, None, ALU.add).then_inc(var[n], 1)

            def minus_mean(n, slot, p):
                dve.wait_ge(rstd[n], slot + 1)
                dve.scalar_tensor_tensor(out=NM[n][p][:, :], in0=MV[n][p][:, :, 0], scalar=-1.0, in1=RS[n][p][:, :],
                                         op0=ALU.mult, op1=ALU.mult).then_inc(nmr[n], 1)

            def both(row):
                return G2[:, row, :].unsqueeze(1).to_broadcast([P, TT, H])

            for g, i, p, where in steps(dve):
                q = 1 - p
                for slot in on_slot(dve, g, 2, where, n_slots):
                    dve.wait_ge(g_act, slot + 1)
                    lo = pair_cols(S[p])[A:P]
                    dve.tensor_tensor(lo, GF[p][A:P, :].rearrange("p (a b t) -> p a b t", a=TT, b=2),
                                      lo.bitcast(F32), ALU.subtract)
                    dve.tensor_copy(pair_cols(X2[p])[0:A], pair_cols(S[p])[0:A].bitcast(F32)).then_inc(s_made, 1)
                for slot in on_slot(dve, g, 3, where, n_slots):
                    minus_mean(1, slot, q)
                for slot in on_slot(dve, g, 0, where, n_slots):
                    dve.wait_ge(z_ps, slot + 1)
                    statistics(0, ZP[p], slot, p)
                for slot in on_slot(dve, g, 3, where, n_slots):
                    dve.wait_ge(n2_act, slot + 1)
                    dve.wait_ge(out_free, slot + 1)
                    dve.tensor_tensor(O[q][:, :, :], N2[q][:, :, :], both(0), ALU.mult).then_inc(o_mul, 1)
                for slot in on_slot(dve, g, 0, where, n_slots):
                    minus_mean(0, slot, p)
                for slot in on_slot(dve, g, 3, where, n_slots):
                    dve.wait_ge(o_mul, slot + 1)
                    dve.tensor_tensor(O[q][:, :, :], O[q][:, :, :], both(1), ALU.add).then_inc(o_made, 1)
                for slot in on_slot(dve, g, 2, where, n_slots):
                    dve.wait_ge(u_ps, slot + 1)
                    statistics(1, UP[p], slot, p)
                if where == HEAD and g == -1:
                    input_high(1, 0, 1)
                    input_low(1, 1)
                else:
                    for slot in on_slot(dve, g, -2, where, n_slots):
                        input_high(slot, i + 1, p)
                    for slot in on_slot(dve, g, -2, where, n_slots):
                        input_low(slot, p)

        @block.scalar
        def _(act):
            for d in range(2):
                act.dma_start(EXP[:, 0:E, d, :], expert_t).then_inc(s_e_in, 16)
            for dst, src in ((UPB[:, :], up_b1), (EB[:, :], expert_b_t), (EM[:, :], emb_t)):
                act.dma_start(dst, src).then_inc(s_e_in, 16)
            act.dma_start(COL[:, :], cols).then_inc(s_col_in, 16)
            for t in range(TT):
                act.dma_start(LB[:, 0:OTHER, t, :], last_b).then_inc(s_lb_in, 16)
            for d in range(2):
                act.dma_start(DD[:, :, d, :], down_t).then_inc(s_col_in, 16)
            act.dma_start(G2[:, :, :], gain2.partition_broadcast(P)).then_inc(s_g2_in, 16)

            def high_half(name):
                act.wait_ge(s_w_in[name], 16)
                act.copy(WH[name], W[name]).then_inc(s_wh[name], 1)

            for name in W:
                high_half(name)
            for j in range(TE // 2):
                bank = UP[j % 2]
                act.wait_ge(s_fold, j + 1)
                act.copy(T1[:, 2 * H * j:2 * H * (j + 1)], flat(bank[:, :, :])).then_inc(s_fold_hi, 1)
            act.wait_ge(s_lb, 1)
            act.dma_start(LBH[1:2, :].bitcast(F32), LBL[:, :].bitcast(F32)).then_inc(s_lb_low, 16)
            act.wait_ge(s_ct, 1)
            act.dma_start(T2[A:A + 1, :].bitcast(F32), CH[:, :].bitcast(F32)).then_inc(s_ct_in, 16)
            act.dma_start(T2[A + 1:A + 2, :].bitcast(F32), CL[:, :].bitcast(F32)).then_inc(s_ct_in, 16)
            act.wait_ge(s_col_in, 48)
            b_sr, b_nr, b_tsr, n_slots = bounds(act)

            def gelu(full, high, src, col, high_ready, full_ready):
                n = len(src)
                for dst, ready in ((high, high_ready), (full, full_ready)):
                    for m in range(n):
                        ins = act.activation(dst[:, m, :], src[m], ACT.Gelu, bias=COL[:, bass.ds(col + m, 1)])
                    ins.then_inc(ready, 1)

            def normalise(n, dst, bank, slot, p, ready):
                act.wait_ge(nmr[n], slot + 1)
                for t in range(TT):
                    ins = act.activation(dst[:, t, :], bank[:, t, :], ACT.Identity, bias=NM[n][p][:, t:t + 1],
                                         scale=RS[n][p][:, t:t + 1])
                ins.then_inc(ready, 1)

            for g, i, p, where in steps(act):
                q = 1 - p
                for slot in on_slot(act, g, 0, where, n_slots):
                    with act.If(g < b_sr):
                        act.wait_ge(h2_ps, g + 1)
                        gelu(h2[:, :, :], h2h[:, :, :], [ZP[p][:, 0, :], ZP[p][:, 1, :]], COL_B2_SR, h2_hi, h2_full)
                for slot in on_slot(act, g, 3, where, n_slots):
                    normalise(1, N2[q], UP[q], slot, q, n2_act)
                for slot in on_slot(act, g, 1, where, n_slots):
                    act.wait_ge(t_ps, slot + 1)
                    for c in range(KC):
                        ins = act.activation(YT[q][:, c, :], TP[:, c, :], ACT.Identity,
                                             bias=COL[:, COL_BETA1 + c:COL_BETA1 + c + 1],
                                             scale=COL[:, COL_G1 + c:COL_G1 + c + 1])
                    ins.then_inc(yt_act, 1)
                with act.If(g + 1 < b_sr):
                    act.wait_ge(h0_ps, g + 2)
                    gelu(h1[:, 0:2, :], h1h[:, 0:2, :], [H0[:, 0, :], H0[:, 1, :]], COL_B1_SR, h0_hi, h0_full)
                    act.wait_ge(h1_ps, g + 2)
                    gelu(h1[:, 2:4, :], h1h[:, 2:4, :], [H1[:, 0, :], H1[:, 1, :]], COL_B1_SR + 2, h1_hi, h1_full)
                with act.Else():
                    for slot in on_slot(act, g, -1, where, n_slots):
                        col = 2 * kind_of(act, slot)
                        act.wait_ge(h0_ps, g + 2)
                        gelu(h2[:, 0:1, :], h2h[:, 0:1, :], [H0[:, 0, :]], col, h0_hi, h0_full)
                        act.wait_ge(h1_ps, g + 2)
                        gelu(h2[:, 1:2, :], h2h[:, 1:2, :], [H1[:, 0, :]], col + 1, h1_hi, h1_full)
                for slot in on_slot(act, g, 1, where, n_slots):
                    act.wait_ge(d_ps, slot + 1)
                    src = DP[:, 0:N].rearrange("p (a b t) -> p a b t", a=TT, b=2)
                    act.activation(pair_cols(S[q]), src, ACT.Gelu, bias=COL[:, COL_DOWN_B:COL_DOWN_B + 1])
                    act.activation(GF[q][A:P, :], DP[A:P, 0:N], ACT.Gelu,
                                   bias=COL[A:P, COL_DOWN_B:COL_DOWN_B + 1]).then_inc(g_act, 1)
                for slot in on_slot(act, g, 0, where, n_slots):
                    normalise(0, ZN, ZP[p], slot, p, zn_act)

        @block.tensor
        def _(pe):
            pe.wait_ge(s_const, 3)
            pe.wait_ge(s_kinds, 1)
            pe.matmul(H0[:, 0, 0:KINDS], before[:, :], kind1[:, :], start=True, stop=True).then_inc(s_rank, 1)
            pe.matmul(H1[:, 0, 0:KINDS], ones[:, :], kind1[:, :], start=True, stop=True).then_inc(s_rank, 1)
            pe.wait_ge(s_placed, 2)
            pe.matmul(ZP[0][0:1, 0, 0:POS], seq_no[:, :], place[:, :], start=True, stop=True).then_inc(s_ids_ps, 1)
            pe.matmul(DP[0:1, 0:POS], ones[:, 0:1], place[:, :], start=True, stop=True)
            pe.matmul(H0[0:1, 1, 0:POS], table_at[:, :], place[:, :], start=True, stop=True)
            pe.matmul(TP[0:1, 1, 0:POS], kind_no[:, :], place[:, :], start=True, stop=True)
            pe.matmul(H1[0:1, 1, 0:POS], ones[:, 0:1], below[:, :], start=True, stop=True).then_inc(s_ids_ps, 1)
            pe.wait_ge(s_weights, 1)
            pe.matmul(TP[0:TE, 0, :], BE[:, :], UPB[:, :], start=True, stop=True).then_inc(s_const_ps, 1)
            for j in range(TE // 2):
                bank = UP[j % 2]
                if j >= 2:
                    pe.wait_ge(s_fold_lo, j - 1)
                for e in range(2):
                    ins = pe.matmul(bank[:, e, :], flat(EXP[:, 2 * j + e, :, :]), UPB[0:A, :], start=True, stop=True)
                ins.then_inc(s_fold, 1)
            pe.wait_ge(s_ids, 1)
            b_sr, b_nr, b_tsr, n_slots = bounds(pe)

            def products(out_ap, lhs, rhs, first, last):
                for n, (a, b) in enumerate(((0, 0), (0, 1), (1, 0))):
                    ins = pe.matmul(out_ap, lhs[a], rhs[b], start=first and n == 0, stop=last and n == 2)
                return ins

            def weight(name, c, cut):
                return WH[name][:, c, cut], WL[name][:, c, cut]

            def weights_ready(where, slot, *names):
                if where == HEAD and slot < 2:
                    for name in names:
                        pe.wait_ge(s_wl[name], 1)

            def first_layer(name, g, p, per_bank):
                for m in range(2 * per_bank):
                    bank, ready = ((H0, h0_ps), (H1, h1_ps))[m // per_bank]
                    for c in range(KC):
                        ins = products(bank[:, m % per_bank, :], weight(name, c, slice(m * P, (m + 1) * P)),
                                       (flat(XH[p][:, :, :, c]), flat(XL[p][:, :, :, c])), c == 0, c == KC - 1)
                    if m % per_bank == per_bank - 1:
                        ins.then_inc(ready, 1)

            def residual(bank, source):
                for t in range(TT):
                    for c in range(KC):
                        ins = pe.matmul(bank[:, t, c * P:(c + 1) * P], source(t, c), ident[:, :],
                                        start=(t == 0 and c == 0), stop=False,
                                        is_transpose=True)
                return ins

            def bank_free(slot):
                if not (isinstance(slot, int) and slot == 0):
                    pe.wait_ge(zn_act, slot)

            def input_tile(p):
                return lambda t, c: flat(XF[p][:, 2 * t:2 * t + 2, :, c])

            def last_layer(kind, highs, lows, p):
                residual(ZP[p], lambda t, c: flat(XF[p][:, 2 * t:2 * t + 2, :, c])).then_inc(x_used, 1)
                pe.matmul(flat(ZP[p][:, :, :]), ones2[:, :], LBH[:, bass.ds(kind * (TT * H), TT * H)],
                          start=False, stop=False)

                def rows(half, c):
                    return half[:, bass.ds(kind * (KC * H) + c * H, H)]

                highs()
                for t in range(TT):
                    for c in range(KC):
                        for half in (last_hi, last_lo):
                            pe.matmul(ZP[p][:, t, :], h2h[:, c, t * P:(t + 1) * P], rows(half, c),
                                      start=False, stop=False)
                lows()
                for t in range(TT):
                    for c in range(KC):
                        ins = pe.matmul(ZP[p][:, t, :], h2l[:, c, t * P:(t + 1) * P], rows(last_hi, c),
                                        start=False, stop=(t == TT - 1 and c == KC - 1))
                ins.then_inc(z_ps, 1)

            def transposes(slot, where):
                if where == HEAD and slot == 0:
                    pe.wait_ge(s_ct, 1)
                pe.wait_ge(zn_act, slot + 1)
                for c in range(KC):
                    for t in range(TT):
                        ins = pe.transpose(TP[:, c, t * P:(t + 1) * P], ZN[:, t, c * P:(c + 1) * P], ident[:, :])
                ins.then_inc(t_ps, 1)

            def expert(slot, p, where):
                at = four(pe, 2, slot, (TE - 1) * H)
                if where == HEAD and slot == 0:
                    pe.wait_ge(s_ct_in, 32)
                    pe.wait_ge(s_fold_lo, TE // 2)
                    pe.wait_ge(s_stack, 2)
                if where != HEAD or slot >= 2:
                    pe.wait_ge(n2_act, slot - 1)
                residual(UP[p], lambda t, c: YT[p][:, c, t * P:(t + 1) * P])
                pe.wait_ge(s_made, slot + 1)
                for t in range(TT):
                    for d in range(2):
                        for stack, table in ((S[p], T1), (X2[p], T2)):
                            ins = pe.matmul(UP[p][:, t, :], flat(stack[:, t, :, :])[:, d * T:d * T + P],
                                            table[:, bass.ds(at[2 * t + d], H)], start=False,
                                            stop=(table is T2 and t == TT - 1 and d == 1))
                ins.then_inc(u_ps, 1)

            def adapter(g, p, where):
                for slot in on_slot(pe, g, 1, where, n_slots):
                    transposes(slot, where)
                for slot in on_slot(pe, g, 2, where, n_slots):
                    expert(slot, p, where)

            def start_layer_0(name, g, q, per_bank, where):
                for slot in on_slot(pe, g, -1, where, n_slots):
                    weights_ready(where, g + 1, name)
                    pe.wait_ge(x_hi, g + 2)
                    pe.wait_ge(x_lo, g + 2)
                    first_layer(name, g, q, per_bank)

            def finish_sr(g, p, where):
                weights_ready(where, g, "w2_sr")
                if where != HEAD or g >= 2:
                    pe.wait_ge(zn_act, g - 1)
                for half, (high, low) in enumerate(((h0_hi, h0_lo), (h1_hi, h1_lo))):
                    chunks = (2 * half, 2 * half + 1)
                    pe.wait_ge(high, g + 1)
                    for m in range(KC):
                        for c in chunks:
                            for n, w in enumerate(weight("w2_sr", c, slice(m * P, (m + 1) * P))):
                                pe.matmul(ZP[p][:, m, :], w, h1h[:, c, :], start=(m == c == n == 0), stop=False)
                    pe.wait_ge(low, g + 1)
                    for m in range(KC):
                        for c in chunks:
                            ins = pe.matmul(ZP[p][:, m, :], WH["w2_sr"][:, c, m * P:(m + 1) * P], h1l[:, c, :],
                                            start=False, stop=(m == KC - 1 and c == 2 * KC - 1))
                ins.then_inc(h2_ps, 1)
                adapter(g, p, where)
                weights_ready(where, g, "w3_sr")
                pe.wait_ge(h2_full, g + 1)
                last_layer(SR, lambda: None, lambda: pe.wait_ge(h2_lo, g + 1), p)

            def finish_other(g, p, where):
                for slot in on_slot(pe, g, 0, where, n_slots):
                    kind = kind_of(pe, slot)
                    weights_ready(where, g, "w2_nr", "w2_tsr")
                    if where != HEAD or g >= 2:
                        pe.wait_ge(zn_act, g - 1)

                    def highs():
                        pe.wait_ge(h0_hi, g + 1)
                        pe.wait_ge(h1_hi, g + 1)

                    def lows():
                        pe.wait_ge(h0_lo, g + 1)
                        pe.wait_ge(h1_lo, g + 1)

                    last_layer(kind, highs, lows, p)
                adapter(g, p, where)

            def by_next_kind(g, q, where, before):
                with pe.If(g + 1 < b_nr):
                    before()
                    start_layer_0("w1_nr", g, q, 1, where)
                with pe.Else():
                    before()
                    start_layer_0("w1_tsr", g, q, 1, where)

            for g, i, p, where in steps(pe):
                q = 1 - p
                if where == HEAD and g == 0:
                    pe.wait_ge(s_lb_low, 16)
                    pe.wait_ge(s_zero_last, 1)
                if where == HEAD and g == 1:
                    for name in W:
                        pe.wait_ge(s_wl[name], 1)
                if where == HEAD and g < 0:
                    with pe.If(b_sr > 0):
                        start_layer_0("w1_sr", g, q, 2, where)
                    with pe.Else():
                        by_next_kind(g, q, where, lambda: None)
                else:
                    with pe.If(g < b_sr):
                        finish_sr(g, p, where)
                        with pe.If(g + 1 < b_sr):
                            start_layer_0("w1_sr", g, q, 2, where)
                        with pe.Else():
                            by_next_kind(g, q, where, lambda: None)
                    with pe.Else():
                        by_next_kind(g, q, where, lambda: finish_other(g, p, where))
                for slot in on_slot(pe, g, 1, where, n_slots):
                    pe.wait_ge(yt_act, slot + 1)
                    for c in range(KC):
                        ins = pe.matmul(DP[:, 0:N], flat(DD[:, c, :, :]), YT[q][:, c, :],
                                        start=(c == 0), stop=(c == KC - 1))
                    ins.then_inc(d_ps, 1)


def kernel(**inputs):
    import numpy as np
    import concourse.bacc as bacc
    from concourse.bass_utils import run_bass_kernel_spmd as run

    v = {k: np.ascontiguousarray(a) for k, a in inputs.items()}
    x = v["x"]
    B, T, H = x.shape
    KC = H // P
    PADDING = 3 * KINDS

    def halves(name):
        return v[name].reshape(-1, P).T

    down_b = v["L1_cond_down_b"]
    data = {
        "x_feat": x.reshape(B, T, KC, P).transpose(0, 3, 1, 2),
        "cond": v["itok_B_0_2"].reshape(B, 1),
        "dom": v["itok_B_0_15"].reshape(B, 1),
        "w1_nr": v["L0_cond_w1_nr"], "w2_nr": v["L0_cond_w2_nr"],
        "w1_tsr": v["L0_cond_w1_tsr"], "w2_tsr": v["L0_cond_w2_tsr"],
        "w1_sr": v["L0_cond_w1_sr"], "w2_sr": v["L0_cond_w2_sr"], "w3_sr": v["L0_cond_w3_sr"],
        "cols": np.concatenate([halves("L0_cond_b2_sr"), halves("L0_cond_b1_nr"), halves("L0_cond_b1_tsr"),
                                halves("L0_cond_b1_sr"), halves("L0_cond_gamma"), halves("L0_cond_beta"),
                                np.concatenate([down_b, down_b]).reshape(P, 1)], axis=1),
        "last_b": np.stack([v["L0_cond_b3_sr"], v["L0_cond_b2_nr"], v["L0_cond_b2_tsr"]])[None],
        "gain2": np.stack([v["L1_cond_ln_gamma"], v["L1_cond_ln_beta"]]),
        "down_t": v["L1_cond_down_W"].T.reshape(KC, P, -1).transpose(1, 0, 2),
        "up_b1": np.concatenate([v["L1_cond_up_W"].T, v["L1_cond_up_b"][None]], axis=0),
        "expert_t": v["L1_cond_expert_W"].transpose(1, 0, 2),
        "expert_b_t": v["L1_cond_expert_b"].T,
        "emb_t": v["L1_cond_domain_emb"].T,
    }
    nc = bacc.Bacc("TRN2", target_bir_lowering=False, num_devices=1)
    arrays, args = {}, []
    for name, a in data.items():
        a = np.ascontiguousarray(a)
        arrays[f"in_{name}"] = a
        args.append(nc.dram_tensor(f"in_{name}", a.shape, mybir.dt.from_np(a.dtype), kind="ExternalInput").ap())
    args.append(nc.dram_tensor("out_0", (B + PADDING, T, H), F32, kind="ExternalOutput").ap())
    conditioned_layers(nc, *args)
    r = run(nc, [arrays], core_ids=[0])
    return r.results[0]["out_0"][:B]
```

```python
from contextlib import ExitStack

import concourse.bass as bass
from concourse import mybir

F32 = mybir.dt.float32
F32R = mybir.dt.float32r
I32 = mybir.dt.int32
ALU = mybir.AluOpType
ACT = mybir.ActivationFunctionType
AX = mybir.AxisListType

P = 128
EPS = 1e-5

SR, NR, TSR, OTHER = range(4)
KINDS = 4
COL_B2_SR, COL_B1_NR, COL_B1_TSR, COL_B1_SR, COL_G1, COL_BETA1, COL_DOWN_B, COLS = 0, 2, 4, 6, 10, 12, 14, 15


def conditioned_layers(nc, x_feat, cond_dom, w1_sr, w2_sr, w1_two, last_w, last_b, per_feature, per_unit, out):
    B, _, T, KC = x_feat.shape
    H = KC * P
    A = per_unit.shape[0] - 1
    E = (per_unit.shape[1] - H) // (2 + 2 * A)
    TE = E + 2
    G = 4
    N = G * T
    TT = N // P
    S_MIN = B // G
    S_MAX = S_MIN + KINDS - 1
    POS = (S_MAX + 1) * G
    WIDTH = POS + 6 * G
    assert B == P and 2 * T == P and 2 * A == P and TT == 2 and KC == 2
    assert out.shape[0] == B + KINDS * (G - 1)

    with ExitStack() as ctx:
        def sb(name, shape, dt=F32):
            return ctx.enter_context(nc.sbuf_tensor(name, shape, dt))

        def ps(name, shape):
            return ctx.enter_context(nc.psum_tensor(name, shape, F32))

        def sem(name):
            return ctx.enter_context(nc.semaphore(name))

        W_DRAM = {"w1_sr": w1_sr, "w2_sr": w2_sr, "last": last_w, "w1_two": w1_two}
        W_COLS = {name: w.shape[1] for name, w in W_DRAM.items()}
        LW = KC * H
        W = {n: sb(n + "_sb", [P, c]) for n, c in W_COLS.items()}
        WH = {n: sb(n + "_hi", [P, c + LW * (n == "last")], F32R) for n, c in W_COLS.items()}
        WL = {n: sb(n + "_lo", [P, c + LW * (n == "last")], F32R) for n, c in W_COLS.items()}
        FEAT = sb("per_feature_sb", [P, COLS + KC * 2 * A + 2 * H])
        COL = FEAT[:, 0:COLS]
        DD = FEAT[:, COLS:COLS + KC * 2 * A].rearrange("p (c m) -> p c m", c=KC)
        G2 = FEAT[:, COLS + KC * 2 * A:].rearrange("p (v n) -> p v n", v=2)
        UNIT = sb("per_unit_sb", [A + 1, H + 2 * E + TE * 2 * A])
        UPB = UNIT[:, 0:H]
        EB = UNIT[0:A, H:H + E]
        EM = UNIT[0:A, H + E:H + 2 * E]
        EXP = UNIT[0:A, H + 2 * E:].rearrange("p (e m) -> p e m", e=TE)
        LB = sb("last_b_sb", [1, KINDS, TT, H])
        LBH = sb("last_b_hi", [2, KINDS * TT * H], F32R)
        LBL = sb("last_b_lo", [1, KINDS * TT * H], F32R)
        IDI = sb("ids_i", [P, 2], I32)
        ident = sb("ident", [P, P])
        before = sb("before", [P, P])
        ones = sb("ones", [P, P])
        ones2 = sb("ones2", [2, P], F32R)
        seq_no = sb("seq_no", [P, 1])
        pos_no = sb("pos_no", [P, POS])
        sc = sb("sort_scratch", [P, 40])
        kind1 = sb("kind_onehot", [P, KINDS])
        start = sb("kind_start", [P, KINDS + 1])
        nslot_i = sb("kind_slots_i", [P, KINDS], I32)
        nslot_s = sb("kind_slots_s", [P, KINDS], I32)
        table_at = sb("table_at", [P, 1])
        kind_no = sb("kind_no", [P, 1])
        place = sb("place", [P, POS])
        below = sb("below", [P, POS])
        pad = sb("pad_scratch", [1, 4, POS])
        MOVES = sb("moves", [1, POS // G + 6, 2 * G], I32)
        IDS = sb("ids", [1, 2, WIDTH], I32)
        BND = sb("bounds", [1, KINDS], I32)
        BE = sb("expert_const", [A + 1, TE])
        CH = sb("const_hi", [TE, H], F32R)
        CL = sb("const_lo", [TE, H], F32R)
        T1 = sb("table_hi", [P, TE * H], F32R)
        T2 = sb("table_lo", [A + 2, TE * H], F32R)
        mhalf = sb("minus_half", [P, TT])
        XF = [sb(f"x{p}", [P, G, T, KC]) for p in range(2)]
        XH = [sb(f"x_hi{p}", [P, G, T, KC], F32R) for p in range(2)]
        XL = [sb(f"x_lo{p}", [P, G, T, KC], F32R) for p in range(2)]
        h1 = sb("h1", [P, 2 * KC, N])
        h1h = sb("h1_hi", [P, 2 * KC, N], F32R)
        h1l = sb("h1_lo", [P, 2 * KC, N], F32R)
        h2 = sb("h2", [P, KC, N])
        h2h = sb("h2_hi", [P, KC, N], F32R)
        h2l = sb("h2_lo", [P, KC, N], F32R)
        ZN = sb("zn", [P, TT, H])
        YT = [sb(f"yt{p}", [P, KC, N]) for p in range(2)]
        GF = [sb(f"gelu_f{p}", [P, N]) for p in range(2)]
        S = [sb(f"stack{p}", [P, TT, 3, T], F32R) for p in range(2)]
        X2 = [sb(f"stack_hi{p}", [A + 2, TT, 3, T], F32R) for p in range(2)]
        N2 = [sb(f"n{p}", [P, TT, H]) for p in range(2)]
        O = [sb(f"o{p}", [P, TT, H]) for p in range(2)]
        ST = [[sb(f"st{n}{p}", [P, TT, 6]) for p in range(2)] for n in range(2)]
        MV = [[sb(f"mv{n}{p}", [P, TT, 2]) for p in range(2)] for n in range(2)]
        VE = [[sb(f"ve{n}{p}", [P, TT]) for p in range(2)] for n in range(2)]
        RS = [[sb(f"rs{n}{p}", [P, TT]) for p in range(2)] for n in range(2)]
        NM = [[sb(f"nm{n}{p}", [P, TT]) for p in range(2)] for n in range(2)]

        H0 = ps("ps_h0", [P, 2, N])
        H1 = ps("ps_h1", [P, 2, N])
        ZP = [ps(f"ps_z{p}", [P, TT, H]) for p in range(2)]
        TP = ps("ps_t", [P, KC, N])
        DP = ps("ps_d", [P, 2 * N])
        UP = [ps(f"ps_u{p}", [P, TT, H]) for p in range(2)]

        s_ids_in = sem("s_ids_in")
        s_feat_in = sem("s_feat_in")
        s_lb_in = sem("s_lb_in")
        s_w_in = {n: sem("in_" + n) for n in W}
        s_wh = {n: sem("hi_" + n) for n in W}
        s_wl = {n: sem("lo_" + n) for n in W}
        s_unit_in = sem("s_unit_in")
        s_const = sem("s_const")
        s_prep = sem("s_prep")
        s_kinds = sem("s_kinds")
        s_zero_last = sem("s_zero_last")
        s_placed = sem("s_placed")
        s_weights = sem("s_weights")
        s_rank = sem("s_rank")
        s_ids_ps = sem("s_ids_ps")
        s_load_ids = sem("s_load_ids")
        s_ids = sem("s_ids")
        s_const_ps = sem("s_const_ps")
        s_ct = sem("s_ct")
        s_ct_in = sem("s_ct_in")
        s_lb = sem("s_lb")
        s_lb_low = sem("s_lb_low")
        s_fold = sem("s_fold")
        s_fold_hi = sem("s_fold_hi")
        s_fold_lo = sem("s_fold_lo")
        s_stack = sem("s_stack")
        ld_x = [sem(f"ld_x{p}") for p in range(2)]
        st_out = [sem(f"st_out{p}") for p in range(2)]
        stored = sem("stored")
        x_hi = sem("x_hi")
        x_lo = sem("x_lo")
        x_used = sem("x_used")
        h0_ps = sem("h0_ps")
        h1_ps = sem("h1_ps")
        h2_ps = sem("h2_ps")
        h0_hi = sem("h0_hi")
        h1_hi = sem("h1_hi")
        h2_hi = sem("h2_hi")
        h0_full = sem("h0_full")
        h1_full = sem("h1_full")
        h2_full = sem("h2_full")
        h0_lo = sem("h0_lo")
        h1_lo = sem("h1_lo")
        h2_lo = sem("h2_lo")
        z_ps = sem("z_ps")
        stat = [sem("stat1"), sem("stat2")]
        stats_seen = sem("stats_seen")
        var = [sem("var1"), sem("var2")]
        rstd = [sem("rstd1"), sem("rstd2")]
        nmr = [sem("nmr1"), sem("nmr2")]
        zn_act = sem("zn_act")
        t_ps = sem("t_ps")
        yt_act = sem("yt_act")
        d_ps = sem("d_ps")
        g_act = sem("g_act")
        s_made = sem("s_made")
        u_ps = sem("u_ps")
        n2_act = sem("n2_act")
        o_mul = sem("o_mul")
        o_made = sem("o_made")

        HEAD, MAIN, LATE, DRAIN = "head", "main", "late", "drain"
        HEAD_STEPS = 4
        TAIL_START = S_MIN - S_MIN % 2 - 2
        LAST_STEP = S_MAX + 4
        EARLY_PAIRS = 3
        PAIRS_IN_STEP = {-1: (3, 4), 0: (5, 6), 1: (7, 8)}
        assert TE == 2 * 9

        def steps(eng, n_slots, last_lag):
            for g in range(-1, HEAD_STEPS):
                yield g, g // 2, g % 2, HEAD
            with eng.Fori(HEAD_STEPS // 2, TAIL_START // 2) as i:
                for p in range(2):
                    yield 2 * i + p, i, p, MAIN
            with eng.Fori(TAIL_START // 2, (LAST_STEP + 1) // 2) as i:
                for p in range(2):
                    with eng.If(2 * i + p < n_slots):
                        yield 2 * i + p, i, p, LATE
                    with eng.Else():
                        with eng.If(2 * i + p < n_slots + last_lag):
                            yield 2 * i + p, i, p, DRAIN

        def pairs(where, g):
            return PAIRS_IN_STEP.get(g, ()) if where == HEAD else ()

        def table_bank(j):
            return DP[:, :].rearrange("p (e n) -> p e n", e=2) if j == 2 else UP[j % 2][:, :, :]

        def on_slot(eng, g, lag, where, n_slots):
            if (where == LATE and lag < 0) or (where == DRAIN and lag > 0):
                with eng.If(g < n_slots + lag):
                    yield g - lag
            elif where in (MAIN, LATE) or (where == HEAD and g >= lag):
                yield g - lag

        def bounds(eng):
            eng.wait_ge(s_load_ids, 1)
            _, v = nc.values_load_multi_w_load_instructions(
                BND[0:1, 0:KINDS], engines=[eng.engine], min_val=0, max_val=S_MAX,
                skip_runtime_bounds_check_because="sums of counts that add up to the number of sequences")
            return v

        def values(eng, ap, top):
            _, v = nc.values_load_multi_w_load_instructions(
                ap, engines=[eng.engine], min_val=0, max_val=top,
                skip_runtime_bounds_check_because="the entries are worked out from one-hot sums")
            return v

        flat_moves = MOVES[:, :, :].rearrange("a s m -> a (s m)")

        def kind_of(eng, slot):
            return values(eng, IDS[0:1, 1, bass.ds(slot * G, 1)], OTHER)[0]

        def pair_cols(tile):
            return tile[:, :, 0:3:2, :]

        def flat(ap):
            return ap.rearrange("p a n -> p (a n)")

        block = ctx.enter_context(nc.Block())

        @block.sync
        def _(sp):
            sp.dma_start(IDI[:, :], cond_dom).then_inc(s_ids_in, 16)
            for name in W:
                sp.dma_start(W[name][:, :], W_DRAM[name]).then_inc(s_w_in[name], 16)

            def load(ids, p):
                for k in range(G):
                    src = x_feat[bass.ds(ids[k], 1), :, :, :].rearrange("a p t c -> (a p) t c")
                    sp.dma_start(XF[p][:, k, :, :], src).then_inc(ld_x[p], 16)

            def rows_to_load(slot):
                return values(sp, flat_moves[:, bass.ds(slot * 2 * G, G)], B - 1)

            def rows_to_store(slot):
                return values(sp, flat_moves[:, bass.ds((slot + 5) * 2 * G + G, G)], out.shape[0] - 1)

            sp.wait_ge(s_load_ids, 1)
            for p in range(2):
                load(rows_to_load(p), p)
            n_slots = bounds(sp)[OTHER]
            sp.wait_ge(s_lb, 1)
            sp.dma_start(LBH[1:2, :].bitcast(F32), LBL[:, :].bitcast(F32)).then_inc(s_lb_low, 16)
            sp.wait_ge(s_ct, 1)
            sp.dma_start(T2[A:A + 1, :].bitcast(F32), CH[:, :].bitcast(F32)).then_inc(s_ct_in, 16)
            sp.dma_start(T2[A + 1:A + 2, :].bitcast(F32), CL[:, :].bitcast(F32)).then_inc(s_ct_in, 16)
            sp.wait_ge(s_ids, 1)
            for g, i, p, where in steps(sp, n_slots, 4):
                q = 1 - p
                if where == HEAD and g < 0:
                    continue
                if where == MAIN:
                    rows = values(sp, flat_moves[:, bass.ds((g + 2) * 2 * G, 2 * G)], out.shape[0] - 1)
                    to_load = [nc.s_assert_within(row, 0, B - 1, skip_runtime_bounds_check_because="an input's row")
                               for row in rows[0:G]]
                    to_store = rows[G:2 * G]
                for slot in on_slot(sp, g, -2, where, n_slots):
                    rows = to_load if where == MAIN else rows_to_load(slot)
                    sp.wait_ge(x_used, g + 1)
                    load(rows, p)
                for slot in on_slot(sp, g, 3, where, n_slots):
                    rows = to_store if where == MAIN else rows_to_store(slot)
                    sp.wait_ge(o_made, slot + 1)
                    for k in range(G):
                        sp.dma_start(out[bass.ds(rows[k], 1), :, :].rearrange("a t n -> (a t) n"),
                                     O[q][T * (k % 2):T * (k % 2) + T, k // 2, :]).then_inc(st_out[q], 16)
                if where in (LATE, DRAIN):
                    for slot in on_slot(sp, g, 4, where, n_slots):
                        sp.wait_ge(st_out[p], 16 * G * (i - 1))
                        sp.sem_inc(stored, 1)

        @block.gpsimd
        def _(pool):
            pool.memset(ones[:, :], 1.0)
            pool.memset(ident[:, :], 0.0).then_inc(s_const, 1)
            pool.iota(seq_no[:, :], pattern=[[0, 1]], base=0, channel_multiplier=1,
                      allow_small_or_imprecise_dtypes=True)
            pool.iota(pos_no[:, :], pattern=[[1, POS]], base=0, channel_multiplier=0,
                      allow_small_or_imprecise_dtypes=True).then_inc(s_const, 1)
            pool.wait_ge(s_const, 2)
            pool.affine_select(out=before[:, :], in_=ones[:, :], compare_op=ALU.is_gt, fill=0.0, base=0,
                               pattern=[[1, P]], channel_multiplier=-1)
            pool.affine_select(out=ident[:, :], in_=ident[:, :], compare_op=ALU.not_equal, fill=1.0, base=0,
                               pattern=[[-1, P]], channel_multiplier=1)
            pool.memset(mhalf[:, :], -0.5).then_inc(s_const, 1)

            for name in W:
                cut = slice(0, W_COLS[name])
                pool.wait_ge(s_wh[name], 1)
                pool.tensor_tensor(WL[name][:, cut], W[name][:, :], WH[name][:, cut].bitcast(F32),
                                   ALU.subtract).then_inc(s_wl[name], 1)
            b_sr, _, _, n_slots = bounds(pool)

            def low(dst, full, high, made, ready, g):
                pool.wait_ge(made, g + 1)
                pool.tensor_tensor(dst, full, high.bitcast(F32), ALU.subtract).then_inc(ready, 1)

            def power(n, slot, p):
                pool.wait_ge(var[n], slot + 1)
                pool.tensor_tensor(RS[n][p][:, :], VE[n][p][:, :], mhalf[:, :], ALU.pow).then_inc(rstd[n], 1)

            for g, i, p, where in steps(pool, n_slots, 3):
                q = 1 - p

                def last_power():
                    for slot in on_slot(pool, g, 3, where, n_slots):
                        power(1, slot, q)

                if where == DRAIN:
                    last_power()
                    continue
                with pool.If(g < b_sr):
                    for slot in on_slot(pool, g, 0, where, n_slots):
                        low(h1l[:, 0:2, :], h1[:, 0:2, :], h1h[:, 0:2, :], h0_full, h0_lo, g)
                        low(h1l[:, 2:4, :], h1[:, 2:4, :], h1h[:, 2:4, :], h1_full, h1_lo, g)
                        last_power()
                        low(h2l[:, :, :], h2[:, :, :], h2h[:, :, :], h2_full, h2_lo, g)
                        power(0, slot, p)
                with pool.Else():
                    for slot in on_slot(pool, g, 0, where, n_slots):
                        low(h2l[:, 0, :], h2[:, 0, :], h2h[:, 0, :], h0_full, h0_lo, g)
                        low(h2l[:, 1, :], h2[:, 1, :], h2h[:, 1, :], h1_full, h1_lo, g)
                    last_power()
                    for slot in on_slot(pool, g, 0, where, n_slots):
                        power(0, slot, p)

        @block.vector
        def _(dve):
            done = [0]

            def step(ins):
                done[0] += 1
                ins.then_inc(s_prep, 1)
                dve.wait_ge(s_prep, done[0])

            C, D, LO, HI = sc[:, 0:1], sc[:, 1:2], sc[:, 2:3], sc[:, 3:4]
            for half in (WH["last"], WL["last"]):
                ins = dve.memset(half[:, OTHER * LW:].bitcast(F32), 0.0)
            ins.then_inc(s_zero_last, 1)
            for p in range(2):
                dve.memset(S[p][:, :, :, :].bitcast(F32), 0.0)
                step(dve.memset(X2[p][:, :, :, :].bitcast(F32), 0.0))
                dve.memset(X2[p][A:A + 2, :, 0:3:2, :].bitcast(F32), 1.0).then_inc(s_stack, 1)
            dve.memset(BE[A:A + 1, :], 1.0)
            dve.memset(ones2[:, :].bitcast(F32), 1.0)
            dve.memset(LB[:, OTHER, :, :], 0.0)
            dve.memset(start[:, 0:1], 0.0)
            dve.wait_ge(s_ids_in, 16)
            step(dve.tensor_copy(sc[:, 0:2], IDI[:, :]))
            dve.tensor_scalar(kind1[:, SR:SR + 1], C, 2.0, None, ALU.is_equal)
            dve.tensor_scalar(kind1[:, NR:NR + 1], C, 0.0, None, ALU.is_equal)
            step(dve.tensor_scalar(kind1[:, TSR:TSR + 1], C, 1.0, None, ALU.is_equal))
            step(dve.tensor_reduce(sc[:, 4:5], kind1[:, 0:OTHER], AX.X, ALU.add))
            dve.tensor_scalar(kind1[:, OTHER:KINDS], sc[:, 4:5], -1.0, 1.0, ALU.mult, ALU.add).then_inc(s_kinds, 1)
            dve.tensor_scalar(LO, D, 0.0, None, ALU.is_lt)
            dve.tensor_scalar(HI, D, float(E), None, ALU.is_ge)
            step(dve.tensor_scalar(sc[:, 5:6], D, 0.0, float(E), ALU.max, ALU.min))
            step(dve.scalar_tensor_tensor(out=sc[:, 6:7], in0=LO, scalar=float(E), in1=sc[:, 5:6],
                                          op0=ALU.mult, op1=ALU.add))
            step(dve.tensor_tensor(sc[:, 7:8], sc[:, 6:7], HI, ALU.add))
            dve.scalar_tensor_tensor(out=sc[:, 30:31], in0=kind1[:, TSR:TSR + 1], scalar=2.0,
                                     in1=kind1[:, NR:NR + 1], op0=ALU.mult, op1=ALU.add)
            step(dve.tensor_scalar(table_at[:, :], sc[:, 7:8], float(H), None, ALU.mult))
            step(dve.scalar_tensor_tensor(out=kind_no[:, :], in0=kind1[:, OTHER:KINDS], scalar=float(OTHER),
                                          in1=sc[:, 30:31], op0=ALU.mult, op1=ALU.add))
            dve.wait_ge(s_rank, 2)
            step(dve.tensor_scalar(nslot_i[:, :], H1[:, 0, 0:KINDS], float(G - 1), None, ALU.add))
            step(dve.tensor_scalar(nslot_s[:, :], nslot_i[:, :], G.bit_length() - 1, None, ALU.arith_shift_right))
            dve.tensor_copy(sc[:, 8:9], nslot_s[:, 0:1])
            step(dve.tensor_tensor(sc[:, 9:8 + KINDS], nslot_s[:, 1:KINDS], nslot_s[:, 0:KINDS - 1], ALU.add))
            dve.tensor_copy(start[:, 1:3], sc[:, 8:10])
            step(dve.tensor_tensor(start[:, 3:1 + KINDS], sc[:, 10:8 + KINDS], sc[:, 8:6 + KINDS], ALU.add))
            dve.tensor_copy(BND[:, :], start[0:1, 1:KINDS + 1])
            step(dve.scalar_tensor_tensor(out=sc[:, 16:16 + KINDS], in0=start[:, 0:KINDS], scalar=float(G),
                                          in1=H0[:, 0, 0:KINDS], op0=ALU.mult, op1=ALU.add))
            step(dve.tensor_tensor(sc[:, 20:20 + KINDS], sc[:, 16:16 + KINDS], kind1[:, :], ALU.mult))
            step(dve.tensor_reduce(sc[:, 24:25], sc[:, 20:20 + KINDS], AX.X, ALU.add))
            dve.wait_ge(s_const, 3)
            dve.tensor_scalar(place[:, :], pos_no[:, :], sc[:, 24:25], None, ALU.is_equal).then_inc(s_placed, 1)
            dve.tensor_scalar(below[:, :], pos_no[:, :], sc[:, 24:25], None, ALU.is_gt).then_inc(s_placed, 1)
            dve.wait_ge(s_ids_ps, 1)
            by_slot = "a (s k) -> a s k"
            dve.tensor_copy(MOVES[:, 0:POS // G, 0:G],
                            ZP[0][0:1, 0, 0:POS].rearrange(by_slot, k=G)).then_inc(s_load_ids, 1)
            dve.wait_ge(s_unit_in, 16)
            dve.tensor_tensor(BE[0:A, 0:E], EB, EM, ALU.add)
            dve.tensor_copy(BE[0:A, E:E + 1], EM[:, 0:1])
            dve.tensor_copy(BE[0:A, E + 1:E + 2], EM[:, E - 1:E])
            for e in (E, E + 1):
                for d in range(2):
                    last = dve.tensor_copy(EXP[:, e, d * A:(d + 1) * A], ident[0:A, 0:A])
            last.then_inc(s_weights, 1)

            def table_low(j):
                bank = table_bank(j)
                at = slice(2 * H * j, 2 * H * (j + 1))
                dve.wait_ge(s_fold_hi, j + 1)
                dve.tensor_tensor(T2[0:A, at], flat(bank[0:A]), T1[0:A, at].bitcast(F32),
                                  ALU.subtract).then_inc(s_fold_lo, 1)

            table_low(0)
            dve.wait_ge(s_ids_ps, 2)
            step(dve.tensor_scalar(pad[:, 0, :], H1[0:1, 1, 0:POS], -1.0, float(B), ALU.mult, ALU.add))
            step(dve.tensor_tensor(pad[:, 1, :], pad[:, 0, :], pos_no[0:1, :], ALU.add))
            step(dve.tensor_tensor(pad[:, 2, :], ZP[1][0:1, 1, 0:POS], pad[:, 1, :], ALU.mult))
            step(dve.tensor_tensor(pad[:, 3, :], pad[:, 1, :], pad[:, 2, :], ALU.subtract))
            step(dve.tensor_tensor(MOVES[:, 5:5 + POS // G, G:2 * G], ZP[0][0:1, 0, 0:POS].rearrange(by_slot, k=G),
                                   pad[:, 3, :].rearrange(by_slot, k=G), ALU.add))
            dve.tensor_copy(IDS[:, 1, 0:POS], ZP[1][0:1, 0, 0:POS])
            dve.tensor_copy(IDS[:, 0, 0:POS], H0[0:1, 1, 0:POS]).then_inc(s_ids, 1)

            n_slots = bounds(dve)[OTHER]

            def input_high(slot, i, p):
                dve.wait_ge(ld_x[p], 16 * G * (i + 1))
                dve.tensor_copy(XH[p][:, :, :, :], XF[p][:, :, :, :]).then_inc(x_hi, 1)

            def input_low(slot, p):
                dve.wait_ge(x_hi, slot + 1)
                dve.tensor_tensor(XL[p][:, :, :, :], XF[p][:, :, :, :], XH[p][:, :, :, :].bitcast(F32),
                                  ALU.subtract).then_inc(x_lo, 1)

            input_high(0, 0, 0)
            input_low(0, 0)
            for j in range(1, EARLY_PAIRS):
                table_low(j)
            dve.wait_ge(s_lb_in, 16)
            lb = LB[:, :, :, :].rearrange("p k t n -> p (k t n)")
            step(dve.tensor_copy(LBH[0:1, :], lb))
            dve.tensor_tensor(LBL[:, :], lb, LBH[0:1, :].bitcast(F32), ALU.subtract).then_inc(s_lb, 1)
            dve.wait_ge(s_const_ps, 1)
            step(dve.tensor_copy(CH[:, :], TP[0:TE, 0, :]))
            dve.tensor_tensor(CL[:, :], TP[0:TE, 0, :], CH[:, :].bitcast(F32), ALU.subtract).then_inc(s_ct, 1)

            def statistics(n, bank, slot, p):
                for t in range(TT):
                    dve.bn_stats(ST[n][p][:, t, :], bank[:, t, :]).then_inc(stat[n], 1)
                dve.wait_ge(stat[n], 2 * TT * slot + TT)
                dve.sem_inc(stats_seen, 1)
                for t in range(TT):
                    dve.bn_aggr(MV[n][p][:, t, :], ST[n][p][:, t, :]).then_inc(stat[n], 1)
                dve.wait_ge(stat[n], 2 * TT * slot + 2 * TT)
                dve.tensor_scalar(VE[n][p][:, :], MV[n][p][:, :, 1], EPS, None, ALU.add).then_inc(var[n], 1)

            def minus_mean(n, slot, p):
                dve.wait_ge(rstd[n], slot + 1)
                dve.scalar_tensor_tensor(out=NM[n][p][:, :], in0=MV[n][p][:, :, 0], scalar=-1.0, in1=RS[n][p][:, :],
                                         op0=ALU.mult, op1=ALU.mult).then_inc(nmr[n], 1)

            def both(row):
                return G2[:, row, :].unsqueeze(1).to_broadcast([P, TT, H])

            def last_gain(g, i, p, where):
                q = 1 - p
                for slot in on_slot(dve, g, 3, where, n_slots):
                    dve.wait_ge(n2_act, slot + 1)
                    if where != HEAD or slot >= 2:
                        dve.wait_ge(st_out[q], 16 * G * (i - 2 if p == 0 else i - 1))
                    dve.tensor_tensor(O[q][:, :, :], N2[q][:, :, :], both(0), ALU.mult).then_inc(o_mul, 1)

            def last_offset(g, p, where):
                q = 1 - p
                for slot in on_slot(dve, g, 3, where, n_slots):
                    dve.wait_ge(o_mul, slot + 1)
                    dve.tensor_tensor(O[q][:, :, :], O[q][:, :, :], both(1), ALU.add).then_inc(o_made, 1)

            for g, i, p, where in steps(dve, n_slots, 3):
                q = 1 - p
                for j in pairs(where, g):
                    table_low(j)
                for slot in on_slot(dve, g, 3, where, n_slots):
                    minus_mean(1, slot, q)
                for slot in on_slot(dve, g, 0, where, n_slots):
                    dve.wait_ge(z_ps, slot + 1)
                    statistics(0, ZP[p], slot, p)
                last_gain(g, i, p, where)
                for slot in on_slot(dve, g, 0, where, n_slots):
                    minus_mean(0, slot, p)
                last_offset(g, p, where)
                for slot in on_slot(dve, g, 2, where, n_slots):
                    dve.wait_ge(u_ps, slot + 1)
                    statistics(1, UP[p], slot, p)
                for slot in on_slot(dve, g, 1, where, n_slots):
                    dve.wait_ge(g_act, slot + 1)
                    lo = pair_cols(S[q])[A:P]
                    dve.tensor_tensor(lo, GF[q][A:P, :].rearrange("p (a b t) -> p a b t", a=TT, b=2),
                                      lo.bitcast(F32), ALU.subtract)
                    dve.tensor_copy(pair_cols(X2[q])[0:A], pair_cols(S[q])[0:A].bitcast(F32)).then_inc(s_made, 1)
                if where == HEAD and g == -1:
                    input_high(1, 0, 1)
                    input_low(1, 1)
                else:
                    for slot in on_slot(dve, g, -2, where, n_slots):
                        input_high(slot, i + 1, p)
                    for slot in on_slot(dve, g, -2, where, n_slots):
                        input_low(slot, p)

        @block.scalar
        def _(act):
            act.dma_start(UNIT[:, 0:per_unit.shape[1]], per_unit).then_inc(s_unit_in, 16)
            act.dma_start(FEAT[:, :], per_feature).then_inc(s_feat_in, 16)
            act.dma_start(LB[:, 0:OTHER, :, :], last_b).then_inc(s_lb_in, 16)
            def table_high(j):
                act.wait_ge(s_fold, j + 1)
                act.copy(T1[:, 2 * H * j:2 * H * (j + 1)], flat(table_bank(j))).then_inc(s_fold_hi, 1)

            for n, name in enumerate(W):
                act.wait_ge(s_w_in[name], 16)
                act.copy(WH[name][:, 0:W_COLS[name]], W[name][:, :]).then_inc(s_wh[name], 1)
                if n < EARLY_PAIRS:
                    table_high(n)

            act.wait_ge(s_feat_in, 16)
            b_sr, _, _, n_slots = bounds(act)
            act.wait_ge(s_ids, 1)

            def gelu(full, high, src, col, high_ready, full_ready):
                n = len(src)
                for dst, ready in ((high, high_ready), (full, full_ready)):
                    for m in range(n):
                        ins = act.activation(dst[:, m, :], src[m], ACT.Gelu, bias=COL[:, bass.ds(col + m, 1)])
                    ins.then_inc(ready, 1)

            def normalise(n, dst, bank, slot, p, ready):
                act.wait_ge(nmr[n], slot + 1)
                for t in range(TT):
                    ins = act.activation(dst[:, t, :], bank[:, t, :], ACT.Identity, bias=NM[n][p][:, t:t + 1],
                                         scale=RS[n][p][:, t:t + 1])
                ins.then_inc(ready, 1)

            for g, i, p, where in steps(act, n_slots, 3):
                q = 1 - p
                for slot in on_slot(act, g, 0, where, n_slots):
                    with act.If(g < b_sr):
                        act.wait_ge(h2_ps, g + 1)
                        gelu(h2[:, :, :], h2h[:, :, :], [ZP[p][:, 0, :], ZP[p][:, 1, :]], COL_B2_SR, h2_hi, h2_full)
                if not (where == HEAD and g < 0):
                    for j in pairs(where, g):
                        table_high(j)
                for slot in on_slot(act, g, 1, where, n_slots):
                    act.wait_ge(t_ps, slot + 1)
                    for c in range(KC):
                        ins = act.activation(YT[q][:, c, :], TP[:, c, :], ACT.Identity,
                                             bias=COL[:, COL_BETA1 + c:COL_BETA1 + c + 1],
                                             scale=COL[:, COL_G1 + c:COL_G1 + c + 1])
                    ins.then_inc(yt_act, 1)
                for slot in on_slot(act, g, 3, where, n_slots):
                    normalise(1, N2[q], UP[q], slot, q, n2_act)
                if where != DRAIN:
                    with act.If(g + 1 < b_sr):
                        act.wait_ge(h0_ps, g + 2)
                        gelu(h1[:, 0:2, :], h1h[:, 0:2, :], [H0[:, 0, :], H0[:, 1, :]], COL_B1_SR, h0_hi, h0_full)
                        act.wait_ge(h1_ps, g + 2)
                        gelu(h1[:, 2:4, :], h1h[:, 2:4, :], [H1[:, 0, :], H1[:, 1, :]], COL_B1_SR + 2, h1_hi, h1_full)
                    with act.Else():
                        for slot in on_slot(act, g, -1, where, n_slots):
                            col = 2 * kind_of(act, slot)
                            act.wait_ge(h0_ps, g + 2)
                            gelu(h2[:, 0:1, :], h2h[:, 0:1, :], [H0[:, 0, :]], col, h0_hi, h0_full)
                            act.wait_ge(h1_ps, g + 2)
                            gelu(h2[:, 1:2, :], h2h[:, 1:2, :], [H1[:, 0, :]], col + 1, h1_hi, h1_full)
                if where == HEAD and g < 0:
                    for j in pairs(where, g):
                        table_high(j)
                for slot in on_slot(act, g, 1, where, n_slots):
                    act.wait_ge(d_ps, slot + 1)
                    src = DP[:, 0:N].rearrange("p (a b t) -> p a b t", a=TT, b=2)
                    act.activation(pair_cols(S[q]), src, ACT.Gelu, bias=COL[:, COL_DOWN_B:COL_DOWN_B + 1])
                    act.activation(GF[q][A:P, :], DP[A:P, 0:N], ACT.Gelu,
                                   bias=COL[A:P, COL_DOWN_B:COL_DOWN_B + 1]).then_inc(g_act, 1)
                for slot in on_slot(act, g, 0, where, n_slots):
                    normalise(0, ZN, ZP[p], slot, p, zn_act)

        @block.tensor
        def _(pe):
            def table_pair(j):
                bank = table_bank(j)
                if j >= EARLY_PAIRS:
                    pe.wait_ge(s_fold_lo, j - 1)
                for e in range(2):
                    ins = pe.matmul(bank[:, e, :], EXP[:, 2 * j + e, :], UPB[0:A, :], start=True, stop=True)
                ins.then_inc(s_fold, 1)

            pe.wait_ge(s_const, 3)
            pe.wait_ge(s_kinds, 1)
            pe.matmul(H0[:, 0, 0:KINDS], before[:, :], kind1[:, :], start=True, stop=True).then_inc(s_rank, 1)
            pe.matmul(H1[:, 0, 0:KINDS], ones[:, :], kind1[:, :], start=True, stop=True).then_inc(s_rank, 1)
            pe.wait_ge(s_unit_in, 16)
            table_pair(0)
            pe.wait_ge(s_placed, 2)
            pe.matmul(ZP[0][0:1, 0, 0:POS], seq_no[:, :], place[:, :], start=True, stop=True).then_inc(s_ids_ps, 1)
            pe.matmul(ZP[1][0:1, 1, 0:POS], ones[:, 0:1], place[:, :], start=True, stop=True)
            pe.matmul(H0[0:1, 1, 0:POS], table_at[:, :], place[:, :], start=True, stop=True)
            pe.matmul(ZP[1][0:1, 0, 0:POS], kind_no[:, :], place[:, :], start=True, stop=True)
            pe.matmul(H1[0:1, 1, 0:POS], ones[:, 0:1], below[:, :], start=True, stop=True).then_inc(s_ids_ps, 1)
            pe.wait_ge(s_weights, 1)
            pe.matmul(TP[0:TE, 0, :], BE[:, :], UPB, start=True, stop=True).then_inc(s_const_ps, 1)
            table_pair(1)
            table_pair(2)
            pe.wait_ge(s_ids, 1)
            b_sr, b_nr, b_tsr, n_slots = bounds(pe)

            def products(out_ap, lhs, rhs, first, last):
                for n, (a, b) in enumerate(((0, 0), (0, 1), (1, 0))):
                    ins = pe.matmul(out_ap, lhs[a], rhs[b], start=first and n == 0, stop=last and n == 2)
                return ins

            def weight(name, row, width, c, m):
                at = slice((row + c) * width + m * P, (row + c) * width + (m + 1) * P)
                return WH[name][:, at], WL[name][:, at]

            def weights_ready(where, slot, *names):
                if where == HEAD and slot < 2:
                    for name in names:
                        pe.wait_ge(s_wl[name], 1)

            def first_layer(name, row, g, p, per_bank):
                for m in range(2 * per_bank):
                    bank, ready = ((H0, h0_ps), (H1, h1_ps))[m // per_bank]
                    for c in range(KC):
                        ins = products(bank[:, m % per_bank, :], weight(name, row, 2 * per_bank * P, c, m),
                                       (flat(XH[p][:, :, :, c]), flat(XL[p][:, :, :, c])), c == 0, c == KC - 1)
                    if m % per_bank == per_bank - 1:
                        ins.then_inc(ready, 1)

            def residual(bank, source):
                for t in range(TT):
                    for c in range(KC):
                        ins = pe.matmul(bank[:, t, c * P:(c + 1) * P], source(t, c), ident[:, :],
                                        start=(t == 0 and c == 0), stop=False,
                                        is_transpose=True)
                return ins

            def bank_free(slot):
                if not (isinstance(slot, int) and slot == 0):
                    pe.wait_ge(zn_act, slot)

            def input_tile(p):
                return lambda t, c: flat(XF[p][:, 2 * t:2 * t + 2, :, c])

            def last_layer(kind, highs, lows, p, first):
                residual(ZP[p], lambda t, c: flat(XF[p][:, 2 * t:2 * t + 2, :, c])).then_inc(x_used, 1)
                if first:
                    pe.wait_ge(s_lb_low, 16)
                pe.matmul(flat(ZP[p][:, :, :]), ones2[:, :], LBH[:, bass.ds(kind * (TT * H), TT * H)],
                          start=False, stop=False)

                def rows(half, c):
                    return half[:, bass.ds(kind * LW + c * H, H)]

                highs()
                for t in range(TT):
                    for c in range(KC):
                        for half in (WH["last"], WL["last"]):
                            pe.matmul(ZP[p][:, t, :], h2h[:, c, t * P:(t + 1) * P], rows(half, c),
                                      start=False, stop=False)
                lows()
                for t in range(TT):
                    for c in range(KC):
                        ins = pe.matmul(ZP[p][:, t, :], h2l[:, c, t * P:(t + 1) * P], rows(WH["last"], c),
                                        start=False, stop=(t == TT - 1 and c == KC - 1))
                ins.then_inc(z_ps, 1)

            def transposes(slot, where):
                if where == HEAD and slot == 0:
                    pe.wait_ge(s_ct, 1)
                pe.wait_ge(zn_act, slot + 1)
                for c in range(KC):
                    for t in range(TT):
                        ins = pe.transpose(TP[:, c, t * P:(t + 1) * P], ZN[:, t, c * P:(c + 1) * P], ident[:, :])
                ins.then_inc(t_ps, 1)

            def expert(slot, p, where):
                at = values(pe, IDS[0:1, 0, bass.ds(slot * G, G)], (TE - 1) * H)
                if where == HEAD and slot == 0:
                    pe.wait_ge(s_ct_in, 32)
                    pe.wait_ge(s_fold_lo, TE // 2)
                    pe.wait_ge(s_stack, 2)
                if where in (LATE, DRAIN):
                    pe.wait_ge(n2_act, slot - 1)
                residual(UP[p], lambda t, c: YT[p][:, c, t * P:(t + 1) * P])
                pe.wait_ge(s_made, slot + 1)
                for t in range(TT):
                    for d in range(2):
                        for stack, table in ((S[p], T1), (X2[p], T2)):
                            ins = pe.matmul(UP[p][:, t, :], flat(stack[:, t, :, :])[:, d * T:d * T + P],
                                            table[:, bass.ds(at[2 * t + d], H)], start=False,
                                            stop=(table is T2 and t == TT - 1 and d == 1))
                ins.then_inc(u_ps, 1)

            def adapter(g, p, where):
                for slot in on_slot(pe, g, 1, where, n_slots):
                    transposes(slot, where)
                for slot in on_slot(pe, g, 2, where, n_slots):
                    expert(slot, p, where)
                for j in pairs(where, g):
                    table_pair(j)

            def start_layer_0(name, row, g, q, per_bank, where):
                for slot in on_slot(pe, g, -1, where, n_slots):
                    weights_ready(where, g + 1, name)
                    pe.wait_ge(x_lo, g + 2)
                    first_layer(name, row, g, q, per_bank)

            def finish_sr(g, p, where):
                weights_ready(where, g, "w2_sr")
                for half, (high, low) in enumerate(((h0_hi, h0_lo), (h1_hi, h1_lo))):
                    chunks = (2 * half, 2 * half + 1)
                    pe.wait_ge(high, g + 1)
                    for m in range(KC):
                        for c in chunks:
                            for n, w in enumerate(weight("w2_sr", 0, H, c, m)):
                                pe.matmul(ZP[p][:, m, :], w, h1h[:, c, :], start=(m == c == n == 0), stop=False)
                    pe.wait_ge(low, g + 1)
                    for m in range(KC):
                        for c in chunks:
                            ins = pe.matmul(ZP[p][:, m, :], weight("w2_sr", 0, H, c, m)[0], h1l[:, c, :],
                                            start=False, stop=(m == KC - 1 and c == 2 * KC - 1))
                ins.then_inc(h2_ps, 1)
                adapter(g, p, where)
                weights_ready(where, g, "last")
                pe.wait_ge(h2_full, g + 1)
                last_layer(SR, lambda: None, lambda: pe.wait_ge(h2_lo, g + 1), p,
                           where == HEAD and g == 0)

            def finish_other(g, p, where):
                for slot in on_slot(pe, g, 0, where, n_slots):
                    kind = kind_of(pe, slot)
                    weights_ready(where, g, "last")
                    last_layer(kind, lambda: pe.wait_ge(h1_hi, g + 1), lambda: pe.wait_ge(h1_lo, g + 1), p,
                               where == HEAD and g == 0)
                adapter(g, p, where)

            def by_next_kind(g, q, where, before):
                with pe.If(g + 1 < b_nr):
                    before()
                    start_layer_0("w1_two", 0, g, q, 1, where)
                with pe.Else():
                    before()
                    start_layer_0("w1_two", KC, g, q, 1, where)

            for g, i, p, where in steps(pe, n_slots, 2):
                q = 1 - p
                if where == HEAD and g == 0:
                    pe.wait_ge(s_zero_last, 1)
                if where == HEAD and g == 1:
                    for name in W:
                        pe.wait_ge(s_wl[name], 1)
                if where == HEAD and g < 0:
                    with pe.If(b_sr > 0):
                        start_layer_0("w1_sr", 0, g, q, 2, where)
                    with pe.Else():
                        by_next_kind(g, q, where, lambda: None)
                elif where == DRAIN:
                    adapter(g, p, where)
                else:
                    with pe.If(g >= b_sr):
                        by_next_kind(g, q, where, lambda: finish_other(g, p, where))
                    with pe.Else():
                        finish_sr(g, p, where)
                        with pe.If(g + 1 < b_sr):
                            start_layer_0("w1_sr", 0, g, q, 2, where)
                        with pe.Else():
                            by_next_kind(g, q, where, lambda: None)
                if where == HEAD and g < 0:
                    for j in pairs(where, g):
                        table_pair(j)
                for slot in on_slot(pe, g, 1, where, n_slots):
                    pe.wait_ge(yt_act, slot + 1)
                    for c in range(KC):
                        ins = pe.matmul(DP[:, 0:N], DD[:, c, :], YT[q][:, c, :],
                                        start=(c == 0), stop=(c == KC - 1))
                    ins.then_inc(d_ps, 1)


def kernel(**inputs):
    import numpy as np
    import concourse.bacc as bacc
    from concourse.bass_utils import run_bass_kernel_spmd as run

    v = {k: np.ascontiguousarray(a) for k, a in inputs.items()}
    x = v["x"]
    B, T, H = x.shape
    KC = H // P
    PADDING = 3 * KINDS

    def vector(name):
        return v[name].reshape(-1, P).T

    def weights(*names):
        return np.concatenate([v[n].reshape(-1, P, v[n].shape[1]).transpose(1, 0, 2).reshape(P, -1) for n in names],
                              axis=1)

    def every_row(a, rows=P):
        return np.broadcast_to(a.reshape(1, -1), (rows, a.size))

    up = v["L1_cond_up_W"].T
    A, E = v["L1_cond_down_W"].shape[0], v["L1_cond_expert_W"].shape[0]
    down = v["L1_cond_down_W"].T.reshape(KC, P, A).transpose(1, 0, 2)
    down_b = v["L1_cond_down_b"].reshape(A, 1)
    expert = v["L1_cond_expert_W"].transpose(1, 0, 2)
    last_b = np.stack([v["L0_cond_b3_sr"], v["L0_cond_b2_nr"], v["L0_cond_b2_tsr"]])
    per_unit = np.zeros((A + 1, H + 2 * E + 2 * A * E), np.float32)
    per_unit[A, 0:H] = v["L1_cond_up_b"]
    per_unit[0:A] = np.concatenate([up, v["L1_cond_expert_b"].T, v["L1_cond_domain_emb"].T,
                                    np.concatenate([expert, expert], axis=2).reshape(A, -1)], axis=1)
    data = {
        "x_feat": x.reshape(B, T, KC, P).transpose(0, 3, 1, 2),
        "cond_dom": np.stack([v["itok_B_0_2"], v["itok_B_0_15"]], axis=1),
        "w1_sr": weights("L0_cond_w1_sr"),
        "w2_sr": weights("L0_cond_w2_sr"),
        "w1_two": weights("L0_cond_w1_nr", "L0_cond_w1_tsr"),
        "last_w": weights("L0_cond_w3_sr", "L0_cond_w2_nr", "L0_cond_w2_tsr"),
        "last_b": np.stack([last_b, last_b], axis=1)[None],
        "per_feature": np.concatenate([
            vector("L0_cond_b2_sr"), vector("L0_cond_b1_nr"), vector("L0_cond_b1_tsr"), vector("L0_cond_b1_sr"),
            vector("L0_cond_gamma"), vector("L0_cond_beta"), np.concatenate([down_b, down_b], axis=0),
            np.concatenate([down, down], axis=2).reshape(P, -1),
            every_row(v["L1_cond_ln_gamma"]), every_row(v["L1_cond_ln_beta"])], axis=1),
        "per_unit": per_unit,
    }
    nc = bacc.Bacc("TRN2", target_bir_lowering=False, num_devices=1)
    arrays, args = {}, []
    for name, a in data.items():
        a = np.ascontiguousarray(a)
        arrays[f"in_{name}"] = a
        args.append(nc.dram_tensor(f"in_{name}", a.shape, mybir.dt.from_np(a.dtype), kind="ExternalInput").ap())
    args.append(nc.dram_tensor("out_0", (B + PADDING, T, H), F32, kind="ExternalOutput").ap())
    conditioned_layers(nc, *args)
    r = run(nc, [arrays], core_ids=[0])
    return r.results[0]["out_0"][:B]
```
